# Optimizing a Trainium2 kernel written in Bass

```python
import numpy as np
import jax
import jax.numpy as jnp

def _softmax(x, axis=-1):
    return jax.nn.softmax(x, axis=axis)

def _gelu(x):
    return jax.nn.gelu(x, approximate=True)

def _silu(x):
    return jax.nn.silu(x)

def _sigmoid(x):
    return jax.nn.sigmoid(x)

def _layernorm(x, axis=-1, eps=1e-05):
    m = jnp.mean(x, axis=axis, keepdims=True)
    v = jnp.var(x, axis=axis, keepdims=True)
    return (x - m) / jnp.sqrt(v + eps)

def _scatter_add(tgt, idx, src, axis=0):
    return tgt.at[idx].add(src)

def _segment_sum(src, seg, n):
    return jax.ops.segment_sum(src, seg, n)
kernel_name = 'mk_seq_postln_d1_jaxref_r8_59e7ca'

def setup_inputs(seed: int=0):
    np.random.seed(seed)
    _w = jnp.asarray

    def _L0_attn_setup():
        import jax, jax.numpy as jnp
        import numpy as np
        D_MODEL = 128
        D_STATE = 16
        D_CONV = 4
        EXPAND = 2
        D_INNER = D_MODEL * EXPAND

        def _forward(x, W_in, conv_w, conv_b, W_x, A_log, D_param, W_dt, b_dt, W_out):
            B, L, _ = x.shape
            xz = x @ W_in.T
            x_ssm, z = jnp.split(xz, 2, axis=-1)
            xc = jnp.transpose(x_ssm, (0, 2, 1))
            xc = jax.lax.conv_general_dilated(xc, conv_w, window_strides=(1,), padding=[(D_CONV - 1, 0)], feature_group_count=D_INNER, dimension_numbers=('NCH', 'OIH', 'NCH'))
            xc = xc + conv_b[None, :, None]
            x_ssm = jax.nn.silu(jnp.transpose(xc, (0, 2, 1)))
            proj = x_ssm @ W_x.T
            B_ssm = proj[..., :D_STATE]
            C_ssm = proj[..., D_STATE:2 * D_STATE]
            dt = jax.nn.softplus(proj[..., -1:] * W_dt[:, 0] + b_dt)
            A = -jnp.exp(A_log)

            def step(h, inp):
                dt_t, Bt, Ct, xt = inp
                dA = jnp.exp(dt_t[..., None] * A)
                h = dA * h + (xt * dt_t)[..., None] * Bt[:, None, :]
                y = jnp.einsum('bdn,bn->bd', h, Ct)
                return (h, y)
            h0 = jnp.zeros((B, D_INNER, D_STATE), x.dtype)
            inputs = (jnp.transpose(dt, (1, 0, 2)), jnp.transpose(B_ssm, (1, 0, 2)), jnp.transpose(C_ssm, (1, 0, 2)), jnp.transpose(x_ssm, (1, 0, 2)))
            _, ys = jax.lax.scan(step, h0, inputs)
            y = jnp.transpose(ys, (1, 0, 2)) + x_ssm * D_param
            y = y * jax.nn.silu(z)
            return y @ W_out.T
        key = jax.random.key(seed)
        ks = jax.random.split(key, 10)
        B, L = (2, 256)
        x = jax.random.normal(ks[0], (B, L, D_MODEL), jnp.float32)
        W_in = jax.random.normal(ks[1], (2 * D_INNER, D_MODEL), jnp.float32) * (1.0 / np.sqrt(D_MODEL))
        conv_w = jax.random.normal(ks[2], (D_INNER, 1, D_CONV), jnp.float32) * (1.0 / np.sqrt(D_CONV))
        conv_b = jax.random.normal(ks[3], (D_INNER,), jnp.float32) * 0.1
        W_x = jax.random.normal(ks[4], (2 * D_STATE + 1, D_INNER), jnp.float32) * (1.0 / np.sqrt(D_INNER))
        A_log = jnp.log(jnp.abs(jax.random.normal(ks[5], (D_INNER, D_STATE), jnp.float32)) + 0.0001)
        D_param = jnp.ones((D_INNER,), jnp.float32)
        W_dt = jax.random.normal(ks[6], (D_INNER, 1), jnp.float32)
        b_dt = jax.random.normal(ks[7], (D_INNER,), jnp.float32) * 0.1
        W_out = jax.random.normal(ks[8], (D_MODEL, D_INNER), jnp.float32) * (1.0 / np.sqrt(D_INNER))
        return {'x': x, 'W_in': W_in, 'conv_w': conv_w, 'conv_b': conv_b, 'W_x': W_x, 'A_log': A_log, 'D_param': D_param, 'W_dt': W_dt, 'b_dt': b_dt, 'W_out': W_out}
    _L0_attn_in = _L0_attn_setup()

    def _L0_ffn_setup():
        import jax, jax.numpy as jnp
        import numpy as np
        D_IN, D_HID = (128, 512)

        def _ternary(key, shape):
            return jax.random.randint(key, shape, -1, 2).astype(jnp.float32)

        def _tlin(x, w, s):
            return jnp.einsum('bsi,oi->bso', x, w) * s
        key = jax.random.key(seed)
        ks = jax.random.split(key, 12)
        inv = lambda fan: 1.0 / np.sqrt(fan).astype(np.float32)
        return {'x': jax.random.normal(ks[0], (4, 256, D_IN), dtype=jnp.float32), 'w1_w': _ternary(ks[1], (D_HID, D_IN)), 'w1_s': jax.random.uniform(ks[2], (D_HID,), dtype=jnp.float32) * inv(D_IN), 'w2_w': _ternary(ks[3], (D_HID, D_IN)), 'w2_s': jax.random.uniform(ks[4], (D_HID,), dtype=jnp.float32) * inv(D_IN), 'h1_w': _ternary(ks[5], (D_HID, D_HID)), 'h1_s': jax.random.uniform(ks[6], (D_HID,), dtype=jnp.float32) * inv(D_HID), 'h2_w': _ternary(ks[7], (D_HID, D_HID)), 'h2_s': jax.random.uniform(ks[8], (D_HID,), dtype=jnp.float32) * inv(D_HID), 'w3_w': _ternary(ks[9], (D_IN, D_HID)), 'w3_s': jax.random.uniform(ks[10], (D_IN,), dtype=jnp.float32) * inv(D_HID)}
    _L0_ffn_in = _L0_ffn_setup()
    _d = {'L0_attn_x': _L0_attn_in['x'], 'L0_attn_W_in': _L0_attn_in['W_in'], 'L0_attn_conv_w': _L0_attn_in['conv_w'], 'L0_attn_conv_b': _L0_attn_in['conv_b'], 'L0_attn_W_x': _L0_attn_in['W_x'], 'L0_attn_A_log': _L0_attn_in['A_log'], 'L0_attn_D_param': _L0_attn_in['D_param'], 'L0_attn_W_dt': _L0_attn_in['W_dt'], 'L0_attn_b_dt': _L0_attn_in['b_dt'], 'L0_attn_W_out': _L0_attn_in['W_out'], 'L0_ffn_w1_w': _L0_ffn_in['w1_w'], 'L0_ffn_w1_s': _L0_ffn_in['w1_s'], 'L0_ffn_w2_w': _L0_ffn_in['w2_w'], 'L0_ffn_w2_s': _L0_ffn_in['w2_s'], 'L0_ffn_h1_w': _L0_ffn_in['h1_w'], 'L0_ffn_h1_s': _L0_ffn_in['h1_s'], 'L0_ffn_h2_w': _L0_ffn_in['h2_w'], 'L0_ffn_h2_s': _L0_ffn_in['h2_s'], 'L0_ffn_w3_w': _L0_ffn_in['w3_w'], 'L0_ffn_w3_s': _L0_ffn_in['w3_s']}
    _x0 = _d['L0_attn_x']
    _d['L0_attn_x'] = jax.random.normal(jax.random.fold_in(jax.random.key(seed), 1), (32, 256, 128), dtype=_x0.dtype)
    del _x0
    return _d

def reference(L0_attn_x, L0_attn_W_in, L0_attn_conv_w, L0_attn_conv_b, L0_attn_W_x, L0_attn_A_log, L0_attn_D_param, L0_attn_W_dt, L0_attn_b_dt, L0_attn_W_out, L0_ffn_w1_w, L0_ffn_w1_s, L0_ffn_w2_w, L0_ffn_w2_s, L0_ffn_h1_w, L0_ffn_h1_s, L0_ffn_h2_w, L0_ffn_h2_s, L0_ffn_w3_w, L0_ffn_w3_s):

    def _L0_attn_ref(x, W_in, conv_w, conv_b, W_x, A_log, D_param, W_dt, b_dt, W_out):
        import jax, jax.numpy as jnp
        import numpy as np
        D_MODEL = 128
        D_STATE = 16
        D_CONV = 4
        EXPAND = 2
        D_INNER = D_MODEL * EXPAND

        def _forward(x, W_in, conv_w, conv_b, W_x, A_log, D_param, W_dt, b_dt, W_out):
            B, L, _ = x.shape
            xz = x @ W_in.T
            x_ssm, z = jnp.split(xz, 2, axis=-1)
            xc = jnp.transpose(x_ssm, (0, 2, 1))
            xc = jax.lax.conv_general_dilated(xc, conv_w, window_strides=(1,), padding=[(D_CONV - 1, 0)], feature_group_count=D_INNER, dimension_numbers=('NCH', 'OIH', 'NCH'))
            xc = xc + conv_b[None, :, None]
            x_ssm = jax.nn.silu(jnp.transpose(xc, (0, 2, 1)))
            proj = x_ssm @ W_x.T
            B_ssm = proj[..., :D_STATE]
            C_ssm = proj[..., D_STATE:2 * D_STATE]
            dt = jax.nn.softplus(proj[..., -1:] * W_dt[:, 0] + b_dt)
            A = -jnp.exp(A_log)

            def step(h, inp):
                dt_t, Bt, Ct, xt = inp
                dA = jnp.exp(dt_t[..., None] * A)
                h = dA * h + (xt * dt_t)[..., None] * Bt[:, None, :]
                y = jnp.einsum('bdn,bn->bd', h, Ct)
                return (h, y)
            h0 = jnp.zeros((B, D_INNER, D_STATE), x.dtype)
            inputs = (jnp.transpose(dt, (1, 0, 2)), jnp.transpose(B_ssm, (1, 0, 2)), jnp.transpose(C_ssm, (1, 0, 2)), jnp.transpose(x_ssm, (1, 0, 2)))
            _, ys = jax.lax.scan(step, h0, inputs)
            y = jnp.transpose(ys, (1, 0, 2)) + x_ssm * D_param
            y = y * jax.nn.silu(z)
            return y @ W_out.T
        return _forward(x, W_in, conv_w, conv_b, W_x, A_log, D_param, W_dt, b_dt, W_out)

    def _L0_ffn_ref(x, w1_w, w1_s, w2_w, w2_s, h1_w, h1_s, h2_w, h2_s, w3_w, w3_s):
        import jax, jax.numpy as jnp
        import numpy as np
        D_IN, D_HID = (128, 512)

        def _ternary(key, shape):
            return jax.random.randint(key, shape, -1, 2).astype(jnp.float32)

        def _tlin(x, w, s):
            return jnp.einsum('bsi,oi->bso', x, w) * s
        h = jax.nn.silu(_tlin(x, w1_w, w1_s)) * _tlin(x, w2_w, w2_s)
        h = jax.nn.gelu(_tlin(h, h1_w, h1_s), approximate=False)
        h = jax.nn.gelu(_tlin(h, h2_w, h2_s), approximate=False)
        return _tlin(h, w3_w, w3_s)
    x = L0_attn_x
    x = _layernorm(x + _L0_attn_ref(x, L0_attn_W_in, L0_attn_conv_w, L0_attn_conv_b, L0_attn_W_x, L0_attn_A_log, L0_attn_D_param, L0_attn_W_dt, L0_attn_b_dt, L0_attn_W_out), axis=-1)
    x = _layernorm(x + _L0_ffn_ref(x, L0_ffn_w1_w, L0_ffn_w1_s, L0_ffn_w2_w, L0_ffn_w2_s, L0_ffn_h1_w, L0_ffn_h1_s, L0_ffn_h2_w, L0_ffn_h2_s, L0_ffn_w3_w, L0_ffn_w3_s), axis=-1)
    return x

_drawn_inputs = setup_inputs


def setup_inputs(seed=0):
    import zlib

    import numpy as np

    out = dict(_drawn_inputs(seed))
    spreads = {'L0_attn_D_param': (1.0, 0.2)}
    factors = {'L0_ffn_w1_w': 8.0,
     'L0_ffn_w1_s': 8.0,
     'L0_ffn_w2_w': 8.0,
     'L0_ffn_w2_s': 8.0,
     'L0_ffn_h1_w': 8.0,
     'L0_ffn_h1_s': 8.0,
     'L0_ffn_h2_w': 8.0,
     'L0_ffn_h2_s': 8.0,
     'L0_ffn_w3_w': 8.0,
     'L0_ffn_w3_s': 8.0}
    for name, (base, spread) in spreads.items():
        noise = np.random.default_rng([zlib.crc32(name.encode()), seed]).standard_normal(out[name].shape)
        drawn = base * np.exp(spread * noise) if base else spread * noise
        out[name] = jnp.asarray(drawn.astype(out[name].dtype))
    for name, factor in factors.items():
        out[name] = (out[name] * factor).astype(out[name].dtype)
    return out
```

```python
from contextlib import ExitStack

import numpy as np
import concourse.bass as bass
from concourse import mybir

F32 = mybir.dt.float32
F32R = mybir.dt.float32r
ALU = mybir.AluOpType
ACT = mybir.ActivationFunctionType

P = 128
SEQS, SEQ, DM = 32, 256, 128
DI, NS, TAPS = 256, 16, 4
NC = DI // P
HID = 512
NH = HID // P
TB = 512
NT = TB // P
PER = TB // SEQ
NB = SEQS * SEQ // TB
UNITS = NS * NC
RING = 4
QN = 4
NQ = NS // QN
SELS = NS + 1
LO = 32
BROW = 64
EPS = 1e-5
CW, CB, AL, DP, WD, BD = 0, 4, 5, 21, 22, 23
CHP = 24


def build(nc, xT, xtok, win, wx, chp, wout, w1, w2, h1, h2, w3, scales, w3s, ident_in, sel_in, out):
    with ExitStack() as ctx:
        def sb(name, shape, dt=F32):
            return ctx.enter_context(nc.sbuf_tensor(name, shape, dt))

        def sem(name):
            return ctx.enter_context(nc.semaphore(name))

        win_sb = sb("win_sb", [P, 2 * DI])
        wpr = sb("wpr", [P, NC, P])
        wout_sb = sb("wout_sb", [P, NC, DM])
        w1_sb = sb("w1_sb", [P, HID])
        w2_sb = sb("w2_sb", [P, HID])
        h1_sb = sb("h1_sb", [P, NH, HID])
        h2_sb = sb("h2_sb", [P, NH, HID])
        w3_sb = sb("w3_sb", [P, NH, DM])
        w3s_sb = sb("w3s_sb", [P, DM])
        chp_sb = sb("chp_sb", [P, NC, CHP])
        sc_sb = sb("sc_sb", [P, 4, NH])
        negA = sb("negA", [P, NC, NS])
        ident = sb("ident", [P, P])
        diagD = sb("diagD", [P, NC, P])
        sel = sb("sel", [P, SELS, P], F32R)
        mhalf = sb("mhalf", [P, NT])
        xT_sb = sb("xT_sb", [P, 2, TB])
        xtok_sb = sb("xtok_sb", [P, 2, NT, DM])
        conv = sb("conv", [P, NC, TB])
        xs = sb("xs", [P, 2, NC, TB])
        zs = sb("zs", [P, 2, NT, DI])
        cdt = sb("cdt", [P, 2, TB], F32R)
        brow = sb("brow", [P, TB])
        relu = sb("relu", [P, NC, TB])
        soft = sb("soft", [P, NC, TB])
        dt = sb("dt", [P, 2, NC, TB])
        xdt = sb("xdt", [P, 2, NC, TB])
        bbc = sb("bbc", [P, NS, TB])
        dA = sb("dA", [P, RING, TB])
        ub = sb("ub", [P, RING, TB])
        hb = sb("hb", [P, RING, TB])
        pb = sb("pb", [P, RING, TB])
        gy = sb("gy", [P, NT, DI])
        gT = sb("gT", [P, NC, TB])
        r1 = sb("r1", [P, NT, DM])
        x1 = sb("x1", [P, NT, DM])
        x1T = sb("x1T", [P, TB])
        sg = sb("sg", [P, NH, TB])
        hid = sb("hid", [P, NH, TB])
        g1 = sb("g1", [P, NH, TB])
        g2 = hid
        r2 = sb("r2", [P, NT, DM])
        yo = sb("yo", [P, NT, DM])
        st1, mv1, ve1, rs1 = sb("st1", [P, NT, 6]), sb("mv1", [P, NT, 2]), sb("ve1", [P, NT]), sb("rs1", [P, NT])
        st2, mv2, ve2, rs2 = sb("st2", [P, NT, 6]), sb("mv2", [P, NT, 2]), sb("ve2", [P, NT]), sb("rs2", [P, NT])
        taker = sb("taker", [P, 1])
        bscr = nc.dram_tensor("bscr", [2, NS * TB], F32, kind="Internal").ap()

        G = [ctx.enter_context(nc.psum_tensor(f"G{i}", [P, TB], F32)) for i in range(4)]
        Y = [ctx.enter_context(nc.psum_tensor(f"Y{i}", [P, 2, DI], F32)) for i in range(2)]
        CB_ = [ctx.enter_context(nc.psum_tensor(f"C{i}", [P, TB], F32)) for i in range(2)]

        s_wload, s_selload = sem("s_wload"), sem("s_selload")
        s_zero, s_setup, s_aexp, s_aneg = sem("s_zero"), sem("s_setup"), sem("s_aexp"), sem("s_aneg")
        s_xT = [sem("s_xT0"), sem("s_xT1")]
        s_xtok = [sem("s_xtok0"), sem("s_xtok1")]
        s_ip = sem("s_ip")
        s_conv0 = sem("s_conv0")
        s_tap = sem("s_tap")
        s_xs = sem("s_xs")
        s_z = sem("s_z")
        s_zs = sem("s_zs")
        s_pr = sem("s_pr")
        s_cdt = sem("s_cdt")
        s_brow = sem("s_brow")
        s_bst = sem("s_bst")
        s_bbc = [sem(f"s_bbc{q}") for q in range(NQ)]
        s_dtb = sem("s_dtb")
        s_pre = sem("s_pre")
        s_soft = sem("s_soft")
        s_dt = sem("s_dt")
        s_xdt = sem("s_xdt")
        s_dA = sem("s_dA")
        s_u = sem("s_u")
        s_h = sem("s_h")
        s_cb = sem("s_cb")
        s_p = sem("s_p")
        s_y = sem("s_y")
        s_gy = sem("s_gy")
        s_gt = sem("s_gt")
        s_gts = sem("s_gts")
        s_op = sem("s_op")
        s_r1 = sem("s_r1")
        s_l1 = sem("s_l1")
        s_rs1 = sem("s_rs1")
        s_x1 = sem("s_x1")
        s_x1t = sem("s_x1t")
        s_x1s = sem("s_x1s")
        s_ga, s_sg = sem("s_ga"), sem("s_sg")
        s_up, s_hid = sem("s_up"), sem("s_hid")
        s_h1, s_g1 = sem("s_h1"), sem("s_g1")
        s_h2, s_g2 = sem("s_h2"), sem("s_g2")
        s_w3 = sem("s_w3")
        s_r2 = sem("s_r2")
        s_l2, s_rs2, s_yo = sem("s_l2"), sem("s_rs2"), sem("s_yo")
        s_out = sem("s_out")

        NW = 22

        def halves(x):
            return x.rearrange("p (s t) -> p s t", s=PER)

        def rounds(eng, run):
            run(0, 0, False, True, True, False, False)
            run(1, 1, False, True, True, True, False)
            with eng.Fori(0, (NB - 4) // 2) as i:
                run(i * 2 + 2, 0, False, True, True, True, True)
                run(i * 2 + 3, 1, False, True, True, True, True)
            run(NB - 2, 0, False, True, True, True, True)
            run(NB - 1, 1, True, True, False, True, True)
            run(NB, 0, True, False, False, True, True)
            run(NB + 1, 1, True, False, False, False, True)

        block = ctx.enter_context(nc.Block())

        @block.sync
        def _(sp):
            def load_xT(b, par):
                sp.dma_start(xT_sb[:, par, :], xT[:, bass.ts(b, TB)]).then_inc(s_xT[par], 16)

            def broadcast_B(b, par, first):
                sp.wait_ge(s_brow, b + 1)
                sp.dma_start(bscr[par].rearrange("(n t) -> n t", n=NS), brow[BROW:BROW + NS, :]).then_inc(s_bst, 16)
                sp.wait_ge(s_bst, 16 * b + 16)
                for q in range(NQ):
                    if not first:
                        sp.wait_ge(s_u, UNITS * (b - 1) + NC * QN * (q + 1))
                    piece = bscr[par:par + 1, q * QN * TB:(q + 1) * QN * TB]
                    sp.dma_start(bbc[:, q * QN:(q + 1) * QN, :].rearrange("p n t -> p (n t)"),
                                 piece.to_broadcast([P, QN * TB])).then_inc(s_bbc[q], 16)

            sp.dma_start(win_sb[:], win).then_inc(s_wload, 16)
            load_xT(0, 0)
            sp.dma_start(chp_sb[:], chp).then_inc(s_wload, 16)
            load_xT(1, 1)
            sp.dma_start(ident[:], ident_in).then_inc(s_wload, 16)
            sp.dma_start(bbc[:, 0:5, :].rearrange("p n t -> p (n t)")[:, 0:SELS * P],
                         sel_in).then_inc(s_selload, 16)
            sp.wait_ge(s_zero, 2)
            for c in range(NC):
                rows = wx[c * P:(c + 1) * P, :]
                for at, lo, hi in ((0, NS, 2 * NS + 1), (LO, NS, 2 * NS + 1), (BROW, 0, NS)):
                    sp.dma_start(wpr[:, c, at:at + hi - lo], rows[:, lo:hi]).then_inc(s_wload, 16)
            sp.dma_start(wout_sb[:], wout.rearrange("(c p) m -> p c m", p=P)).then_inc(s_wload, 16)
            sp.dma_start(w1_sb[:], w1).then_inc(s_wload, 16)
            sp.dma_start(w2_sb[:], w2).then_inc(s_wload, 16)
            for k in range(2):
                sl = slice(k * NH // 2, (k + 1) * NH // 2)
                sp.dma_start(h1_sb[:, sl, :], h1.rearrange("(c p) m -> p c m", p=P)[:, sl, :]).then_inc(s_wload, 16)
                sp.dma_start(h2_sb[:, sl, :], h2.rearrange("(c p) m -> p c m", p=P)[:, sl, :]).then_inc(s_wload, 16)
            for k in range(NH):
                sp.dma_start(w3_sb[:, k, :], w3[k * P:(k + 1) * P, :]).then_inc(s_wload, 16)
            sp.dma_start(w3s_sb[:], w3s.to_broadcast([P, DM])).then_inc(s_wload, 16)
            sp.dma_start(sc_sb[:], scales).then_inc(s_wload, 16)
            sp.wait_ge(s_setup, 2)
            broadcast_B(0, 0, True)

            def run(j, par, last, scan, front, back, tail):
                if scan and front and not (isinstance(j, int) and j + 2 >= NB):
                    sp.wait_ge(s_z, 2 * j + 2)
                    load_xT(j + 2, par)
                if scan:
                    if back and not (isinstance(j, int) and j < 2):
                        sp.wait_ge(s_r1, j - 1)
                    sp.dma_start(xtok_sb[:, par, :, :],
                                 xtok[bass.ts(j, TB), :].rearrange("(t p) m -> p t m", p=P)).then_inc(s_xtok[par], 16)
                if tail:
                    sp.wait_ge(s_yo, j - 1)
                    sp.dma_start(out[bass.ts(j - 2, TB), :].rearrange("(t p) m -> p t m", p=P),
                                 yo[:]).then_inc(s_out, 16)
                if front:
                    broadcast_B(j + 1, 1 - par, False)

            rounds(sp, run)
            sp.wait_ge(s_out, 16 * NB)

        @block.gpsimd
        def _(pool):
            def dt_and_xdt(b, par):
                for c in range(NC):
                    pool.wait_ge(s_soft, 2 * b + 2)
                    pool.wait_ge(s_pre, 4 * b + 4)
                    nc.gpsimd.tensor_tensor(dt[:, par, c, :], relu[:, c, :], soft[:, c, :], ALU.add).then_inc(s_dt, 1)
                for c in range(NC):
                    pool.wait_ge(s_dt, 2 * b + 1 + c)
                    pool.wait_ge(s_xs, 2 * b + 1 + c)
                    nc.gpsimd.tensor_tensor(xdt[:, par, c, :], dt[:, par, c, :], xs[:, par, c, :],
                                            ALU.mult).then_inc(s_xdt, 1)

            def input_term(b, par, u, first):
                n, c = divmod(u, NC)
                if n == 0:
                    pool.wait_ge(s_xdt, 2 * b + 1 + c)
                if n % QN == 0 and c == 0:
                    pool.wait_ge(s_bbc[n // QN], 16 * b + 16)
                if u >= RING or not first:
                    pool.wait_ge(s_h, UNITS * b + u - RING + 1)
                nc.gpsimd.tensor_tensor(ub[:, u % RING, :], xdt[:, par, c, :], bbc[:, n, :], ALU.mult).then_inc(s_u, 1)

            nc.gpsimd.memset(mhalf[:], -0.5).then_inc(s_zero, 1)
            nc.gpsimd.memset(wpr[:].rearrange("p c n -> p (c n)"), 0.0).then_inc(s_zero, 1)
            dt_and_xdt(0, 0)
            input_term(0, 0, 0, True)
            input_term(0, 0, 1, True)

            def run(j, par, last, scan, front, back, tail):
                first = isinstance(j, int) and j == 0
                for u in range(UNITS):
                    if u + 2 < UNITS and scan:
                        input_term(j, par, u + 2, first)
                    if u + 2 >= UNITS and front:
                        input_term(j + 1, 1 - par, u + 2 - UNITS, False)
                    if u == 3 and tail:
                        pool.wait_ge(s_l2, 3 * (j - 2) + 3)
                        nc.gpsimd.tensor_tensor(rs2[:], ve2[:], mhalf[:], ALU.pow).then_inc(s_rs2, 1)
                    if u == 6 and back:
                        pool.wait_ge(s_l1, 3 * (j - 1) + 3)
                        nc.gpsimd.tensor_tensor(rs1[:], ve1[:], mhalf[:], ALU.pow).then_inc(s_rs1, 1)
                    if u == 19 and front:
                        dt_and_xdt(j + 1, 1 - par)

            rounds(pool, run)

        @block.scalar
        def _(act):
            def decay(b, par, u, first):
                n, c = divmod(u, NC)
                if n == 0:
                    act.wait_ge(s_dt, 2 * b + 1 + c)
                if u >= RING or not first:
                    act.wait_ge(s_h, UNITS * b + u - RING + 1)
                nc.scalar.activation(halves(dA[:, u % RING, :])[:, :, 1:SEQ],
                                     halves(dt[:, par, c, :])[:, :, 1:SEQ], ACT.Exp,
                                     scale=negA[:, c, n:n + 1]).then_inc(s_dA, 1)

            def conv_first(b):
                for c in range(NC):
                    act.wait_ge(s_ip, 2 * b + 1 + c)
                    nc.scalar.activation(conv[:, c, :], G[2 + c][:], ACT.Identity,
                                         bias=chp_sb[:, c, CB:CB + 1],
                                         scale=chp_sb[:, c, CW + TAPS - 1:CW + TAPS]).then_inc(s_conv0, 1)

            def silu_front(b, par):
                for c in range(NC):
                    act.wait_ge(s_tap, 6 * b + 5 + c)
                    nc.scalar.activation(xs[:, par, c, :], conv[:, c, :], ACT.Silu).then_inc(s_xs, 1)
                for i in range(2):
                    act.wait_ge(s_z, 2 * b + 1 + i)
                    nc.scalar.activation(zs[:, par, 2 * i:2 * i + 2, :].rearrange("p t d -> p (t d)"), G[i][:],
                                         ACT.Silu).then_inc(s_zs, 1)

            def copy_B(b, first):
                act.wait_ge(s_pr, b + 1)
                if not first:
                    act.wait_ge(s_bst, 16 * b)
                nc.scalar.activation(brow[BROW:BROW + NS, :], G[2][BROW:BROW + NS, :], ACT.Copy).then_inc(s_brow, 1)

            def softplus_pre(b):
                act.wait_ge(s_dtb, b + 1)
                if not (isinstance(b, int) and b == 0):
                    act.wait_ge(s_dt, 2 * b)
                for c in range(NC):
                    for f, o in ((ACT.Abs, soft), (ACT.Relu, relu)):
                        nc.scalar.activation(o[:, c, :], G[2][:], f, bias=chp_sb[:, c, BD:BD + 1],
                                             scale=chp_sb[:, c, WD:WD + 1]).then_inc(s_pre, 1)

            def softplus_ln(b):
                v = soft[:].rearrange("p c t -> p (c t)")
                act.wait_ge(s_pre, 4 * b + 4)
                nc.scalar.activation(v, v, ACT.Exp, scale=-1.0).then_inc(s_soft, 1)
                act.wait_ge(s_soft, 2 * b + 1)
                nc.scalar.activation(v, v, ACT.Ln, bias=1.0).then_inc(s_soft, 1)

            act.wait_ge(s_wload, 16 * NW)
            for c in range(NC):
                nc.scalar.activation(negA[:, c, :], chp_sb[:, c, AL:AL + NS], ACT.Exp).then_inc(s_aexp, 1)
            act.wait_ge(s_aexp, NC)
            nc.scalar.mul(negA[:].rearrange("p c n -> p (c n)"),
                          negA[:].rearrange("p c n -> p (c n)"), -1.0).then_inc(s_aneg, 1)
            conv_first(0)
            silu_front(0, 0)
            copy_B(0, True)
            softplus_pre(0)
            softplus_ln(0)
            act.wait_ge(s_aneg, 1)
            act.wait_ge(s_setup, 1)
            for u in range(3):
                decay(0, 0, u, True)

            def run(j, par, last, scan, front, back, tail):
                first = isinstance(j, int) and j == 0
                F, A = j - 1, j + 1
                for u in range(UNITS):
                    if u + 3 < UNITS and scan:
                        decay(j, par, u + 3, first)
                    if u + 3 >= UNITS and front:
                        decay(A, 1 - par, u + 3 - UNITS, False)
                    if u == 1 and front:
                        conv_first(A)
                    if u == 2 and back:
                        for c in range(NC):
                            act.wait_ge(s_gt, 2 * F + 1 + c)
                            nc.scalar.activation(gT[:, c, :], G[c][:], ACT.Copy).then_inc(s_gts, 1)
                    if u == 8 and back:
                        act.wait_ge(s_x1t, F + 1)
                        nc.scalar.activation(x1T[:], G[3][:], ACT.Copy).then_inc(s_x1s, 1)
                    if u == 10:
                        if front:
                            silu_front(A, 1 - par)
                        if back:
                            for m in range(NH):
                                act.wait_ge(s_ga, 4 * F + 1 + m)
                                nc.scalar.activation(sg[:, m, :], G[(m + 2) % 4][:], ACT.Silu,
                                                     scale=sc_sb[:, 0, m:m + 1]).then_inc(s_sg, 1)
                    if u == 13 and front:
                        copy_B(A, False)
                    if u == 16 and front:
                        softplus_pre(A)
                    if u == 17 and front:
                        softplus_ln(A)
                    if u == 21 and back:
                        for m in range(NH):
                            act.wait_ge(s_h1, 4 * F + 1 + m)
                            nc.scalar.activation(g1[:, m, :], G[m][:], ACT.Gelu,
                                                 scale=sc_sb[:, 2, m:m + 1]).then_inc(s_g1, 1)
                    if u == 29 and back:
                        for m in range(NH):
                            act.wait_ge(s_h2, 4 * F + 1 + m)
                            nc.scalar.activation(g2[:, m, :], G[m][:], ACT.Gelu,
                                                 scale=sc_sb[:, 3, m:m + 1]).then_inc(s_g2, 1)

            rounds(act, run)

        @block.vector
        def _(dve):
            def taps(b, step):
                for c in range(NC):
                    s = step + 1
                    k = TAPS - 1 - s
                    if step == 0:
                        dve.wait_ge(s_conv0, 2 * b + 1 + c)
                    else:
                        dve.wait_ge(s_tap, 6 * b + 2 * step - 1 + c)
                    acc = halves(conv[:, c, :])[:, :, s:SEQ]
                    nc.vector.scalar_tensor_tensor(out=acc, in0=halves(G[2 + c][:])[:, :, 0:SEQ - s],
                                                   scalar=chp_sb[:, c, CW + k:CW + k + 1], in1=acc,
                                                   op0=ALU.mult, op1=ALU.add).then_inc(s_tap, 1)

            def split(b, par):
                dve.wait_ge(s_pr, b + 1)
                nc.vector.tensor_copy(cdt[0:2 * LO, par, :], G[2][0:2 * LO, :]).then_inc(s_cdt, 1)
                dve.wait_ge(s_cdt, 2 * b + 1)
                low = cdt[LO:2 * LO, par, :]
                nc.vector.tensor_tensor(low, G[2][LO:2 * LO, :], low.bitcast(F32), ALU.subtract).then_inc(s_cdt, 1)

            def stats(r, st, mv, ve, s_r, s_l, b):
                dve.wait_ge(s_r, b + 1)
                for t in range(NT):
                    last = nc.vector.bn_stats(st[:, t, :], r[:, t, :])
                last.then_inc(s_l, 1)
                dve.wait_ge(s_l, 3 * b + 1)
                nc.vector.memset(taker[:], 0.0)
                for t in range(NT):
                    last = nc.vector.bn_aggr(mv[:, t, :], st[:, t, :])
                last.then_inc(s_l, 1)
                dve.wait_ge(s_l, 3 * b + 2)
                nc.vector.tensor_scalar(ve[:], mv[:, :, 1], EPS, None, ALU.add).then_inc(s_l, 1)

            def normalise(o, r, mv, rs, s_rs, s_o, b):
                dve.wait_ge(s_rs, b + 1)
                for t in range(NT):
                    last = nc.vector.tensor_scalar(o[:, t, :], r[:, t, :], mv[:, t, 0:1], rs[:, t:t + 1],
                                                   ALU.subtract, ALU.mult)
                last.then_inc(s_o, 1)

            nc.vector.memset(dA[:].rearrange("p r t -> p (r t)"), 0.0)
            nc.vector.memset(cdt[:].bitcast(F32), 0.0).then_inc(s_setup, 1)
            dve.wait_ge(s_selload, 16)
            nc.vector.tensor_copy(sel[:].rearrange("p n m -> p (n m)"),
                                  bbc[:, 0:5, :].rearrange("p n t -> p (n t)")[:, 0:SELS * P]).then_inc(s_setup, 1)
            dve.wait_ge(s_wload, 16 * NW)
            for c in range(NC):
                nc.vector.tensor_scalar(diagD[:, c, :], ident[:], chp_sb[:, c, DP:DP + 1], None,
                                        ALU.mult).then_inc(s_setup, 1)
            for k in range(NH):
                nc.vector.tensor_tensor(w3_sb[:, k, :], w3_sb[:, k, :], w3s_sb[:], ALU.mult).then_inc(s_setup, 1)
            for step in range(3):
                taps(0, step)
            split(0, 0)

            def run(j, par, last, scan, front, back, tail):
                first = isinstance(j, int) and j == 0
                F, A, T = j - 1, j + 1, j - 2
                for u in range(UNITS + 1):
                    if u < UNITS and scan:
                        dve.wait_ge(s_dA, UNITS * j + u + 1)
                        dve.wait_ge(s_u, UNITS * j + u + 1)
                        nc.vector.tensor_tensor_scan(hb[:, u % RING, :], dA[:, u % RING, :], ub[:, u % RING, :],
                                                     0.0, ALU.mult, ALU.add).then_inc(s_h, 1)
                    if u >= 1 and scan:
                        v = u - 1
                        n, c = divmod(v, NC)
                        dve.wait_ge(s_h, UNITS * j + v + 1)
                        if c == 0:
                            dve.wait_ge(s_cb, NS * j + n + 1)
                        if v >= RING or not first:
                            dve.wait_ge(s_y, UNITS * j + v - RING + 1)
                        nc.vector.tensor_tensor(pb[:, v % RING, :], hb[:, v % RING, :], CB_[n % 2][:],
                                                ALU.mult).then_inc(s_p, 1)
                    if u == 0 and tail:
                        dve.wait_ge(s_w3, T + 1)
                        nc.vector.tensor_tensor(r2[:].rearrange("p t m -> p (t m)"), G[0][:],
                                                x1[:].rearrange("p t m -> p (t m)"), ALU.add).then_inc(s_r2, 1)
                    if u == 1 and back:
                        dve.wait_ge(s_y, UNITS * j)
                        for i in range(2):
                            nc.vector.tensor_tensor(gy[:, 2 * i:2 * i + 2, :], Y[i][:],
                                                    zs[:, 1 - par, 2 * i:2 * i + 2, :], ALU.mult).then_inc(s_gy, 1)
                    if u == 2 and tail:
                        stats(r2, st2, mv2, ve2, s_r2, s_l2, T)
                    if front and 2 <= u < 5:
                        taps(A, u - 2)
                    if u == 4 and tail:
                        if not (isinstance(T, int) and T == 0):
                            dve.wait_ge(s_out, 16 * T)
                        normalise(yo, r2, mv2, rs2, s_rs2, s_yo, T)
                    if u == 5 and back:
                        dve.wait_ge(s_op, F + 1)
                        dve.wait_ge(s_xtok[1 - par], (F - (1 - par)) * 8 + 16)
                        nc.vector.tensor_tensor(r1[:].rearrange("p t m -> p (t m)"), G[2][:],
                                                xtok_sb[:, 1 - par, :, :].rearrange("p t m -> p (t m)"),
                                                ALU.add).then_inc(s_r1, 1)
                        stats(r1, st1, mv1, ve1, s_r1, s_l1, F)
                    if u == 7 and back:
                        normalise(x1, r1, mv1, rs1, s_rs1, s_x1, F)
                    if u == 13 and front:
                        split(A, 1 - par)
                    if 14 <= u < 18 and back:
                        m = u - 14
                        dve.wait_ge(s_up, 4 * F + 1 + m)
                        dve.wait_ge(s_sg, 4 * F + 1 + m)
                        nc.vector.scalar_tensor_tensor(out=hid[:, m, :], in0=G[(3, 0, 1, 3)[m]][:],
                                                       scalar=sc_sb[:, 1, m:m + 1], in1=sg[:, m, :],
                                                       op0=ALU.mult, op1=ALU.mult).then_inc(s_hid, 1)

            rounds(dve, run)

        @block.tensor
        def _(pe):
            def token_tile(x, t):
                return x[:, t * P:(t + 1) * P]

            def in_proj(b, par):
                pe.wait_ge(s_xT[par], (b - par) * 8 + 16)
                for c in range(NC):
                    nc.tensor.matmul(G[2 + c][:], win_sb[:, c * P:(c + 1) * P], xT_sb[:, par, :],
                                     start=True, stop=True).then_inc(s_ip, 1)

            def z_proj(b, par, free):
                for i in range(2):
                    free(i)
                    for t in range(2):
                        last = nc.tensor.matmul(G[i][:, t * DI:(t + 1) * DI],
                                                token_tile(xT_sb[:, par, :], 2 * i + t), win_sb[:, DI:2 * DI],
                                                start=(t == 0), stop=True, skip_group_check=True)
                    last.then_inc(s_z, 1)

            def bcdt_proj(b, par):
                for c in range(NC):
                    pe.wait_ge(s_xs, 2 * b + 1 + c)
                    last = nc.tensor.matmul(G[2][:], wpr[:, c, :], xs[:, par, c, :], start=(c == 0), stop=(c == NC - 1))
                last.then_inc(s_pr, 1)

            def dt_broadcast(b, par):
                pe.wait_ge(s_cdt, 2 * b + 2)
                pe.wait_ge(s_brow, b + 1)
                nc.tensor.matmul(G[2][:], sel[:, NS, :], cdt[:, par, :], start=True, stop=True).then_inc(s_dtb, 1)

            def c_broadcast(b, par, n, first):
                if n >= 2 or not first:
                    pe.wait_ge(s_p, UNITS * b + NC * (n - 1))
                nc.tensor.matmul(CB_[n % 2][:], sel[:, n, :], cdt[:, par, :], start=True, stop=True).then_inc(s_cb, 1)

            def ffn_rows(bank, w, m, ks, x):
                for k in ks:
                    last = nc.tensor.matmul(bank[:], w[:, k, m * P:(m + 1) * P], x[:, k, :],
                                            start=(k == 0), stop=(k == NH - 1))
                return last

            pe.wait_ge(s_wload, 16 * NW)
            in_proj(0, 0)
            z_proj(0, 0, lambda i: None)
            pe.wait_ge(s_tap, 5)
            bcdt_proj(0, 0)
            pe.wait_ge(s_setup, 4 + NH)
            dt_broadcast(0, 0)
            c_broadcast(0, 0, 0, True)

            def run(j, par, last_, scan, front, back, tail):
                first = isinstance(j, int) and j == 0
                F, A, T = j - 1, j + 1, j - 2
                for u in range(UNITS + 2):
                    if u == 1:
                        if back:
                            if tail:
                                pe.wait_ge(s_r2, T + 1)
                                pe.wait_ge(s_g2, 4 * T + 2)
                            else:
                                pe.wait_ge(s_zs, 2 * j + 2)
                            for c in range(NC):
                                for t in range(NT):
                                    pe.wait_ge(s_gy, 2 * F + 1 + t // 2)
                                    last = nc.tensor.transpose(token_tile(G[c], t),
                                                               gy[:, t, c * P:(c + 1) * P], ident[:])
                                last.then_inc(s_gt, 1)
                        if scan:
                            for i in range(2):
                                for t in range(2):
                                    for c in range(NC):
                                        nc.tensor.matmul(Y[i][:, t, c * P:(c + 1) * P],
                                                         token_tile(xs[:, par, c, :], 2 * i + t), diagD[:, c, :],
                                                         start=(t == 0 and c == 0), stop=False, skip_group_check=True)
                    if u >= 2 and scan:
                        v = u - 2
                        c = v % NC
                        pe.wait_ge(s_p, UNITS * j + v + 1)
                        for t in range(NT):
                            last = nc.tensor.matmul(Y[t // 2][:, t % 2, c * P:(c + 1) * P],
                                                    token_tile(pb[:, v % RING, :], t), ident[:], is_transpose=True,
                                                    start=False, stop=(v >= UNITS - NC), skip_group_check=True)
                        last.then_inc(s_y, 1)
                    if u % 2 == 1 and u < UNITS - 1 and scan:
                        c_broadcast(j, par, (u + 1) // 2, first)
                    if u == UNITS - 1 and front:
                        c_broadcast(A, 1 - par, 0, False)
                    if u == 0 and front:
                        if tail:
                            pe.wait_ge(s_g2, 4 * T + 4)
                        else:
                            pe.wait_ge(s_pre, 4 * j + 4)
                            pe.wait_ge(s_tap, 6 * j + 6)
                        in_proj(A, 1 - par)
                    if u == 3 and back:
                        if front:
                            pe.wait_ge(s_tap, 6 * A + 5)
                        else:
                            pe.wait_ge(s_g2, 4 * T + 3)
                        pe.wait_ge(s_gts, 2 * F + 2)
                        for t in range(NT):
                            for c in range(NC):
                                last = nc.tensor.matmul(token_tile(G[2], t), token_tile(gT[:, c, :], t),
                                                        wout_sb[:, c, :], start=(t == 0 and c == 0),
                                                        stop=(c == NC - 1), skip_group_check=True)
                        last.then_inc(s_op, 1)
                    if u == 4 and front:
                        if back:
                            z_proj(A, 1 - par, lambda i: None)
                        else:
                            z_proj(A, 1 - par, lambda i: pe.wait_ge(s_zs, 2 * j + 2))
                    if u == 7 and back:
                        if front:
                            pe.wait_ge(s_tap, 6 * A + 6)
                        else:
                            pe.wait_ge(s_g2, 4 * T + 4)
                        pe.wait_ge(s_x1, F + 1)
                        for t in range(NT):
                            last = nc.tensor.transpose(token_tile(G[3], t), x1[:, t, :], ident[:])
                        last.then_inc(s_x1t, 1)
                    if u in (8, 10) and back:
                        if u == 8:
                            pe.wait_ge(s_r1, F + 1)
                            pe.wait_ge(s_x1s, F + 1)
                        for m in (0, 1) if u == 8 else (2, 3):
                            if m >= 2 and front:
                                pe.wait_ge(s_zs, 2 * A + m - 1)
                            nc.tensor.matmul(G[(m + 2) % 4][:], w1_sb[:, m * P:(m + 1) * P], x1T[:],
                                             start=True, stop=True).then_inc(s_ga, 1)
                    if u == 12 and front:
                        if back:
                            pe.wait_ge(s_sg, 4 * F + 1)
                        else:
                            pe.wait_ge(s_tap, 6 * A + 5)
                        bcdt_proj(A, 1 - par)
                    if u in (12, 13, 14) and back:
                        for m in ((0,), (1, 2), (3,))[u - 12]:
                            if m < 3:
                                pe.wait_ge(s_sg, 4 * F + 2 + m)
                            else:
                                pe.wait_ge(s_hid, 4 * F + 1)
                            nc.tensor.matmul(G[(3, 0, 1, 3)[m]][:], w2_sb[:, m * P:(m + 1) * P], x1T[:],
                                             start=True, stop=True).then_inc(s_up, 1)
                    if u == 15 and front:
                        dt_broadcast(A, 1 - par)
                    if 15 <= u < 23 and back:
                        m, part = divmod(u - 15, 2)
                        if u == 15:
                            pe.wait_ge(s_hid, 4 * F + 4)
                        if m == 2 and part == 0 and front:
                            pe.wait_ge(s_pre, 4 * A + 4)
                        last = ffn_rows(G[m], h1_sb, m, range(2 * part, 2 * part + 2), hid)
                        if part == 1:
                            last.then_inc(s_h1, 1)
                    if 23 <= u < 31 and back:
                        m, part = divmod(u - 23, 2)
                        for k in range(2 * part, 2 * part + 2):
                            pe.wait_ge(s_g1, 4 * F + 1 + max(k, m))
                            last = ffn_rows(G[m], h2_sb, m, (k,), g1)
                        if part == 1:
                            last.then_inc(s_h2, 1)
                    if u == 31 and back:
                        for k in range(NH):
                            pe.wait_ge(s_g2, 4 * F + 1 + k)
                            for t in range(NT):
                                last = nc.tensor.matmul(token_tile(G[0], t), token_tile(g2[:, k, :], t),
                                                        w3_sb[:, k, :], start=(k == 0 and t == 0),
                                                        stop=(k == NH - 1), skip_group_check=True)
                        last.then_inc(s_w3, 1)

            rounds(pe, run)


def kernel(L0_attn_x, L0_attn_W_in, L0_attn_conv_w, L0_attn_conv_b, L0_attn_W_x, L0_attn_A_log, L0_attn_D_param,
           L0_attn_W_dt, L0_attn_b_dt, L0_attn_W_out, L0_ffn_w1_w, L0_ffn_w1_s, L0_ffn_w2_w, L0_ffn_w2_s,
           L0_ffn_h1_w, L0_ffn_h1_s, L0_ffn_h2_w, L0_ffn_h2_s, L0_ffn_w3_w, L0_ffn_w3_s):
    import concourse.bacc as _bacc
    from concourse.bass_utils import run_bass_kernel_spmd as _run

    def arr(a):
        return np.asarray(a)

    def chan(a, k):
        return arr(a).reshape(NC, P, k).transpose(1, 0, 2)

    x = arr(L0_attn_x).reshape(SEQS * SEQ, DM)
    chp = np.concatenate([chan(L0_attn_conv_w, TAPS), chan(L0_attn_conv_b, 1), chan(L0_attn_A_log, NS),
                          chan(L0_attn_D_param, 1), chan(L0_attn_W_dt, 1), chan(L0_attn_b_dt, 1)], axis=2)
    scales = np.stack([arr(s).reshape(NH, P).T for s in (L0_ffn_w1_s, L0_ffn_w2_s, L0_ffn_h1_s, L0_ffn_h2_s)], axis=1)
    sel = np.zeros((P, SELS, P), np.float32)
    for n in range(SELS):
        sel[n, n, :] = 1.0
        sel[LO + n, n, :] = 1.0
    ins = {
        "xT": x.T, "xtok": x, "win": arr(L0_attn_W_in).T, "wx": arr(L0_attn_W_x).T, "chp": chp,
        "wout": arr(L0_attn_W_out).T, "w1": arr(L0_ffn_w1_w).T, "w2": arr(L0_ffn_w2_w).T,
        "h1": arr(L0_ffn_h1_w).T, "h2": arr(L0_ffn_h2_w).T, "w3": arr(L0_ffn_w3_w).T, "scales": scales,
        "w3s": arr(L0_ffn_w3_s).reshape(1, DM), "ident_in": np.eye(P, dtype=np.float32),
        "sel_in": sel.reshape(P, SELS * P),
    }
    nc = _bacc.Bacc("TRN2", target_bir_lowering=False, num_devices=1)
    arrays, args = {}, {}
    for name, a in ins.items():
        arrays[f"{name}_d"] = np.ascontiguousarray(a)
        args[name] = nc.dram_tensor(f"{name}_d", list(a.shape), mybir.dt.from_np(arrays[f"{name}_d"].dtype),
                                    kind="ExternalInput").ap()
    args["out"] = nc.dram_tensor("out_d", [SEQS * SEQ, DM], F32, kind="ExternalOutput").ap()
    build(nc, **args)
    r = _run(nc, [arrays], core_ids=[0])
    return r.results[0]["out_d"].reshape(SEQS, SEQ, DM)
```

```python
from contextlib import ExitStack

import numpy as np
import concourse.bass as bass
from concourse import mybir

F32 = mybir.dt.float32
F32R = mybir.dt.float32r
ALU = mybir.AluOpType
ACT = mybir.ActivationFunctionType

P = 128
SEQS, SEQ, DM = 32, 256, 128
DI, NS, TAPS = 256, 16, 4
NC = DI // P
HID = 512
NH = HID // P
TB = 512
NT = TB // P
PER = TB // SEQ
NB = SEQS * SEQ // TB
UNITS = NS * NC
RING = 8
OUTS = 4
QN = 4
NQ = NS // QN
SELS = NS + 1
LO = 32
BROW = 64
EPS = 1e-5
PE_AT = dict(z=(0, 0), turn_y=1, start_y=(2, 2), out_proj=3, in_proj=(3, 3), turn_x1=6, gate_up=(8, 8, 10, 11),
             bcdt=11, dt_row=13, h1=(16, 17, 18, 19, 20, 21, 22, 23), h2=(25, 25, 25, 27, 28, 29, 30, 30),
             w3=(31, 32))
ACT_AT = dict(z=4, y=4, conv=7, x1=9, silu=11, hid=(12, 12, 13, 15), b_rows=13, soft=15, ln=16,
              gelu1=(17, 17, 21, 21), gelu2=(26, 26, 31, 31))
DVE_AT = dict(r2=1, gate=1, r1=5, taps=(5, 5, 5), x1=5, x1_low=7, hid=(10, 10, 12, 13), cdt=13, stats2=19, yo=20,
              g2=(30, 30, 32, 32))
POOL_AT = dict(rs1=3, hid=(14, 14, 14, 14), dt=23, xdt=26, rs2=19, g1=(20, 20, 21, 21))
ACT_AHEAD, POOL_AHEAD = 4, 5
SUM_LAG = 3
CW, CB, AL, DP, WD, BD = 0, 4, 5, 21, 22, 23
CHP = 24


def build(nc, xT, xtok, win, wx, chp, wout, w1, w2, h1, h2, w3, scales, w3s, ident_in, out):
    with ExitStack() as ctx:
        def sb(name, shape, dt=F32):
            return ctx.enter_context(nc.sbuf_tensor(name, shape, dt))

        def sem(name):
            return ctx.enter_context(nc.semaphore(name))

        win_sb = sb("win_sb", [P, 2 * DI])
        wpr = sb("wpr", [P, NC, P])
        wout_sb = sb("wout_sb", [P, NC, DM])
        w1_hl = sb("w1_hl", [P, 2, 1, HID], F32R)
        w2_hl = sb("w2_hl", [P, 2, 1, HID], F32R)
        h1_hl = sb("h1_hl", [P, 2, NH, HID], F32R)
        h2_hl = sb("h2_hl", [P, 2, NH, HID], F32R)
        w3_hl = sb("w3_hl", [P, 2, NH, DM], F32R)
        w3s_sb = sb("w3s_sb", [P, DM])
        chp_sb = sb("chp_sb", [P, NC, CHP])
        sc_sb = sb("sc_sb", [P, 4, NH])
        negA = sb("negA", [P, NC, NS])
        ident = sb("ident", [P, P])
        diagD = sb("diagD", [P, NC, P])
        sel = sb("sel", [P, SELS, P], F32R)
        mhalf = sb("mhalf", [P, NT])
        xT_sb = sb("xT_sb", [P, TB])
        xtok_sb = sb("xtok_sb", [P, NT, DM])
        conv = sb("conv", [P, NC, TB])
        xs = sb("xs", [P, NC, TB])
        zs = sb("zs", [P, 2, NT, DI])
        cdt = sb("cdt", [P, 2, TB], F32R)
        soft = conv
        dt = sb("dt", [P, 2, NC, TB])
        xdt = sb("xdt", [P, 2, NC, TB])
        brow = xdt[BROW:BROW + NS, :, NC - 1, :]
        bbc = sb("bbc", [P, 2, QN, TB])
        dA = sb("dA", [P, RING, TB])
        ub = sb("ub", [P, RING, TB])
        hb = ub
        pb = sb("pb", [P, OUTS, TB])
        gy = sb("gy", [P, NT, DI])
        gT = conv
        r1 = sb("r1", [P, NT, DM])
        x1 = r1
        relu = gy[:].rearrange("p t d -> p (t d)").rearrange("p (c t) -> p c t", c=NC)
        x1T = sb("x1T", [P, 2, 1, TB], F32R)
        hid = sb("hid", [P, 2, NH, TB], F32R)
        g1 = sb("g1", [P, 2, NH, TB], F32R)
        g2 = hid
        full = sb("full", [P, NH, TB])
        r2 = sb("r2", [P, NT, DM])
        yo = r2
        st1, mv1, ve1, rs1 = sb("st1", [P, NT, 6]), sb("mv1", [P, NT, 2]), sb("ve1", [P, NT]), sb("rs1", [P, NT])
        st2, mv2, ve2, rs2 = sb("st2", [P, NT, 6]), sb("mv2", [P, NT, 2]), sb("ve2", [P, NT]), sb("rs2", [P, NT])
        taker = sb("taker", [P, 1])
        bscr = nc.dram_tensor("bscr", [2, NS * TB], F32, kind="Internal").ap()

        G = [ctx.enter_context(nc.psum_tensor(f"G{i}", [P, TB], F32)) for i in range(4)]
        Y = [ctx.enter_context(nc.psum_tensor(f"Y{i}", [P, 2, DI], F32)) for i in range(2)]
        CB_ = [ctx.enter_context(nc.psum_tensor(f"C{i}", [P, TB], F32)) for i in range(2)]

        s_first, s_proj, s_stage = sem("s_first"), sem("s_proj"), sem("s_stage")
        s_zero, s_const, s_aexp, s_aneg = sem("s_zero"), sem("s_const"), sem("s_aexp"), sem("s_aneg")
        s_w3s = sem("s_w3s")
        s_wsplit = sem("s_wsplit")
        s_xT = sem("s_xT")
        s_xtok = sem("s_xtok")
        s_z = sem("s_z")
        s_zc = sem("s_zc")
        s_zs = sem("s_zs")
        s_ip = sem("s_ip")
        s_conv0 = sem("s_conv0")
        s_tap = sem("s_tap")
        s_xs = sem("s_xs")
        s_pr = sem("s_pr")
        s_cdt = sem("s_cdt")
        s_brow = sem("s_brow")
        s_bst = sem("s_bst")
        s_bbc = [sem(f"s_bbc{q}") for q in range(NQ)]
        s_dtb = sem("s_dtb")
        s_pre = sem("s_pre")
        s_soft = sem("s_soft")
        s_dt = sem("s_dt")
        s_xdt = sem("s_xdt")
        s_dA = sem("s_dA")
        s_u = sem("s_u")
        s_h = sem("s_h")
        s_cb = sem("s_cb")
        s_p = sem("s_p")
        s_y = sem("s_y")
        s_gy = sem("s_gy")
        s_gt = sem("s_gt")
        s_gts = sem("s_gts")
        s_op = sem("s_op")
        s_r1 = sem("s_r1")
        s_l1 = sem("s_l1")
        s_rs1 = sem("s_rs1")
        s_x1 = sem("s_x1")
        s_x1t = sem("s_x1t")
        s_x1h, s_x1l = sem("s_x1h"), sem("s_x1l")
        s_ga, s_sg = sem("s_ga"), sem("s_sg")
        s_up, s_hid = sem("s_up"), sem("s_hid")
        s_hh, s_hl = sem("s_hh"), sem("s_hl")
        s_h1 = sem("s_h1")
        s_g1h, s_g1f, s_g1l = sem("s_g1h"), sem("s_g1f"), sem("s_g1l")
        s_h2 = sem("s_h2")
        s_g2h, s_g2f, s_g2l = sem("s_g2h"), sem("s_g2f"), sem("s_g2l")
        s_w3 = sem("s_w3")
        s_r2 = sem("s_r2")
        s_l2, s_rs2, s_yo = sem("s_l2"), sem("s_rs2"), sem("s_yo")
        s_out = sem("s_out")

        def halves(x):
            return x.rearrange("p (s t) -> p s t", s=PER)

        def flat(x):
            return x.rearrange("p a b -> p (a b)")

        def due(slots, u):
            return [i for i, slot in enumerate(slots) if slot == u]

        def bank(m):
            return G[(m + 1) % 4]

        def rounds(eng, run):
            run(0, 0, True, True, False, False)
            run(1, 1, True, True, True, False)
            with eng.Fori(0, (NB - 4) // 2) as i:
                run(i * 2 + 2, 0, True, True, True, True)
                run(i * 2 + 3, 1, True, True, True, True)
            run(NB - 2, 0, True, True, True, True)
            run(NB - 1, 1, True, False, True, True)
            run(NB, 0, False, False, True, True)
            run(NB + 1, 1, False, False, False, True)

        block = ctx.enter_context(nc.Block())

        @block.sync
        def _(sp):
            def load_xT(b):
                sp.dma_start(xT_sb[:], xT[:, bass.ts(b, TB)]).then_inc(s_xT, 16)

            def store_B(b, par):
                sp.wait_ge(s_brow, b + 1)
                sp.dma_start(bscr[par].rearrange("(n t) -> n t", n=NS), brow[:, par, :]).then_inc(s_bst, 16)

            def broadcast_B(b, par, q, free):
                if free is not None:
                    sp.wait_ge(s_u, free)
                if q == 0:
                    sp.wait_ge(s_bst, 16 * b + 16)
                piece = bscr[par:par + 1, q * QN * TB:(q + 1) * QN * TB]
                sp.dma_start(flat(bbc[:, q % 2, :, :]), piece.to_broadcast([P, QN * TB])).then_inc(s_bbc[q], 16)

            load_xT(0)
            sp.dma_start(win_sb[:], win).then_inc(s_first, 16)
            sp.dma_start(chp_sb[:], chp).then_inc(s_first, 16)
            sp.dma_start(ident[:], ident_in).then_inc(s_first, 16)
            sp.wait_ge(s_zero, 2)
            for c in range(NC):
                rows = wx[c * P:(c + 1) * P, :]
                for at, lo, hi in ((0, NS, 2 * NS + 1), (LO, NS, 2 * NS + 1), (BROW, 0, NS)):
                    sp.dma_start(wpr[:, c, at:at + hi - lo], rows[:, lo:hi]).then_inc(s_proj, 16)
            sp.dma_start(wout_sb[:], wout.rearrange("(c p) m -> p c m", p=P)).then_inc(s_proj, 16)
            sp.dma_start(sc_sb[:], scales).then_inc(s_proj, 16)
            sp.dma_start(w3s_sb[:], w3s.to_broadcast([P, DM])).then_inc(s_proj, 16)
            sp.wait_ge(s_ip, 2)
            sp.wait_ge(s_z, 2)
            load_xT(1)
            sp.dma_start(full[:], h1.rearrange("(c p) m -> p c m", p=P)).then_inc(s_stage, 16)
            store_B(0, 0)
            broadcast_B(0, 0, 0, None)
            broadcast_B(0, 0, 1, None)
            sp.wait_ge(s_wsplit, 2)
            sp.dma_start(full[:], h2.rearrange("(c p) m -> p c m", p=P)).then_inc(s_stage, 16)
            sp.wait_ge(s_wsplit, 4)
            sp.dma_start(full[:, 0, :], w1).then_inc(s_stage, 16)
            sp.dma_start(full[:, 1, :], w2).then_inc(s_stage, 16)
            sp.dma_start(full[:, 2, :].rearrange("p (c m) -> p c m", c=NH),
                         w3.rearrange("(c p) m -> p c m", p=P)).then_inc(s_stage, 16)

            def run(j, par, scan, front, back, tail):
                F, A, T = j - 1, j + 1, j - 2
                if front and not (isinstance(j, int) and j + 2 >= NB):
                    sp.wait_ge(s_ip, 2 * A + 2)
                    load_xT(j + 2)
                if scan:
                    if back:
                        sp.wait_ge(s_r1, F + 1)
                    sp.dma_start(xtok_sb[:], xtok[bass.ts(j, TB), :].rearrange("(t p) m -> p t m", p=P)).then_inc(s_xtok, 16)
                    broadcast_B(j, par, 2, UNITS * j + NC * QN)
                if front:
                    store_B(A, 1 - par)
                if scan:
                    broadcast_B(j, par, 3, UNITS * j + 2 * NC * QN)
                if front:
                    broadcast_B(A, 1 - par, 0, UNITS * j + 3 * NC * QN)
                if tail:
                    sp.wait_ge(s_yo, T + 1)
                    sp.dma_start(out[bass.ts(T, TB), :].rearrange("(t p) m -> p t m", p=P),
                                 yo[:]).then_inc(s_out, 16)
                if front:
                    broadcast_B(A, 1 - par, 1, UNITS * j + 4 * NC * QN)

            rounds(sp, run)
            sp.wait_ge(s_out, 16 * NB)

        @block.gpsimd
        def _(pool):
            def add_dt(b, par):
                for c in range(NC):
                    pool.wait_ge(s_soft, 2 * b + 2)
                    nc.gpsimd.tensor_tensor(dt[:, par, c, :], relu[:, c, :], soft[:, c, :], ALU.add).then_inc(s_dt, 1)

            def mult_xdt(b, par):
                for c in range(NC):
                    pool.wait_ge(s_dt, 2 * b + 1 + c)
                    pool.wait_ge(s_xs, 2 * b + 1 + c)
                    if c == NC - 1:
                        pool.wait_ge(s_bst, 16 * b + 16)
                    nc.gpsimd.tensor_tensor(xdt[:, par, c, :], dt[:, par, c, :], xs[:, c, :],
                                            ALU.mult).then_inc(s_xdt, 1)

            def input_term(b, par, u, first):
                n, c = divmod(u, NC)
                if n == 0:
                    pool.wait_ge(s_xdt, 2 * b + 1 + c)
                if n % QN == 0 and c == 0:
                    pool.wait_ge(s_bbc[n // QN], 16 * b + 16)
                if u >= RING or not first:
                    pool.wait_ge(s_p, UNITS * b + u - RING + 1)
                nc.gpsimd.tensor_tensor(ub[:, u % RING, :], xdt[:, par, c, :], bbc[:, n // QN % 2, n % QN, :],
                                        ALU.mult).then_inc(s_u, 1)

            def low(x, m, s_full, s_low, b):
                pool.wait_ge(s_full, 4 * b + 1 + m)
                nc.gpsimd.tensor_tensor(x[:, 1, m, :], full[:, m, :], x[:, 0, m, :].bitcast(F32),
                                        ALU.subtract).then_inc(s_low, 1)

            nc.gpsimd.memset(mhalf[:], -0.5).then_inc(s_zero, 1)
            nc.gpsimd.memset(flat(wpr[:]), 0.0).then_inc(s_zero, 1)
            add_dt(0, 0)
            mult_xdt(0, 0)
            for u in range(POOL_AHEAD):
                input_term(0, 0, u, True)

            def run(j, par, scan, front, back, tail):
                first = isinstance(j, int) and j == 0
                F, A, T = j - 1, j + 1, j - 2
                at = POOL_AT
                for u in range(UNITS):
                    ahead = u + POOL_AHEAD
                    if ahead < UNITS and scan:
                        input_term(j, par, ahead, first)
                    if ahead >= UNITS and front:
                        input_term(A, 1 - par, ahead - UNITS, False)
                    if u == at["rs1"] and back:
                        pool.wait_ge(s_l1, 3 * F + 3)
                        nc.gpsimd.tensor_tensor(rs1[:], ve1[:], mhalf[:], ALU.pow).then_inc(s_rs1, 1)
                    if back:
                        for m in due(at["hid"], u):
                            low(hid, m, s_hh, s_hl, F)
                    if u == at["dt"] and front:
                        add_dt(A, 1 - par)
                    if u == at["xdt"] and front:
                        mult_xdt(A, 1 - par)
                    if u == at["rs2"] and tail:
                        pool.wait_ge(s_l2, 3 * T + 3)
                        nc.gpsimd.tensor_tensor(rs2[:], ve2[:], mhalf[:], ALU.pow).then_inc(s_rs2, 1)
                    if back:
                        for m in due(at["g1"], u):
                            low(g1, m, s_g1f, s_g1l, F)

            rounds(pool, run)

        @block.scalar
        def _(act):
            def decay(b, par, u, first):
                n, c = divmod(u, NC)
                if n == 0:
                    act.wait_ge(s_dt, 2 * b + 1 + c)
                if u >= RING or not first:
                    act.wait_ge(s_h, UNITS * b + u - RING + 1)
                nc.scalar.activation(halves(dA[:, u % RING, :])[:, :, 1:SEQ],
                                     halves(dt[:, par, c, :])[:, :, 1:SEQ], ACT.Exp,
                                     scale=negA[:, c, n:n + 1]).then_inc(s_dA, 1)

            def copy_z(b, par, back):
                if back:
                    act.wait_ge(s_gy, 2 * (b - 2) + 2)
                for i in range(2):
                    act.wait_ge(s_z, 2 * b + 1 + i)
                    nc.scalar.activation(flat(zs[:, par, 2 * i:2 * i + 2, :]), G[i][:], ACT.Copy).then_inc(s_zc, 1)

            def conv_first(b):
                for c in range(NC):
                    act.wait_ge(s_ip, 2 * b + 1 + c)
                    nc.scalar.activation(conv[:, c, :], G[2 + c][:], ACT.Identity,
                                         bias=chp_sb[:, c, CB:CB + 1],
                                         scale=chp_sb[:, c, CW + TAPS - 1:CW + TAPS]).then_inc(s_conv0, 1)

            def silu_conv(b, par):
                for c in range(NC):
                    act.wait_ge(s_tap, 6 * b + 5 + c)
                    nc.scalar.activation(xs[:, c, :], conv[:, c, :], ACT.Silu).then_inc(s_xs, 1)

            def silu_z(b, par):
                act.wait_ge(s_zc, 2 * b + 2)
                for i in range(2):
                    z = flat(zs[:, par, 2 * i:2 * i + 2, :])
                    nc.scalar.activation(z, z, ACT.Silu).then_inc(s_zs, 1)

            def silu_gate(b, m):
                act.wait_ge(s_ga, 4 * b + 1 + m)
                nc.scalar.activation(full[:, m, :], G[m % 2][:], ACT.Silu,
                                     scale=sc_sb[:, 0, m:m + 1]).then_inc(s_sg, 1)

            def gelu(x, kind, s_in, s_high, s_full, b, ms):
                for m in ms:
                    act.wait_ge(s_in, 4 * b + 1 + m)
                    scale = sc_sb[:, kind, m:m + 1]
                    nc.scalar.activation(x[:, 0, m, :], bank(m)[:], ACT.Gelu, scale=scale).then_inc(s_high, 1)
                    nc.scalar.activation(full[:, m, :], bank(m)[:], ACT.Gelu, scale=scale).then_inc(s_full, 1)

            def copy_B(b, par):
                act.wait_ge(s_pr, b + 1)
                nc.scalar.activation(brow[:, par, :], G[0][BROW:BROW + NS, :], ACT.Copy).then_inc(s_brow, 1)

            def softplus_pre(b):
                act.wait_ge(s_dtb, b + 1)
                for c in range(NC):
                    for f, o in ((ACT.Abs, soft), (ACT.Relu, relu)):
                        nc.scalar.activation(o[:, c, :], G[0][:], f, bias=chp_sb[:, c, BD:BD + 1],
                                             scale=chp_sb[:, c, WD:WD + 1]).then_inc(s_pre, 1)

            def softplus_ln(b):
                v = flat(soft[:])
                act.wait_ge(s_pre, 4 * b + 4)
                nc.scalar.activation(v, v, ACT.Exp, scale=-1.0).then_inc(s_soft, 1)
                act.wait_ge(s_soft, 2 * b + 1)
                nc.scalar.activation(v, v, ACT.Ln, bias=1.0).then_inc(s_soft, 1)

            act.wait_ge(s_first, 16 * 3)
            conv_first(0)
            copy_z(0, 0, False)
            silu_conv(0, 0)
            silu_z(0, 0)
            copy_B(0, 0)
            softplus_pre(0)
            softplus_ln(0)
            for c in range(NC):
                nc.scalar.activation(negA[:, c, :], chp_sb[:, c, AL:AL + NS], ACT.Exp).then_inc(s_aexp, 1)
            act.wait_ge(s_aexp, NC)
            nc.scalar.mul(flat(negA[:]), flat(negA[:]), -1.0).then_inc(s_aneg, 1)
            act.wait_ge(s_aneg, 1)
            act.wait_ge(s_const, 1)
            for u in range(ACT_AHEAD):
                decay(0, 0, u, True)

            def run(j, par, scan, front, back, tail):
                first = isinstance(j, int) and j == 0
                F, A = j - 1, j + 1
                at = ACT_AT
                for u in range(UNITS):
                    ahead = u + ACT_AHEAD
                    if ahead < UNITS and scan:
                        decay(j, par, ahead, first)
                    if ahead >= UNITS and front:
                        decay(A, 1 - par, ahead - UNITS, False)
                    if u == at["z"] and front:
                        copy_z(A, 1 - par, back)
                    if u == at["y"] and back:
                        for c in range(NC):
                            act.wait_ge(s_gt, 2 * F + 1 + c)
                            nc.scalar.activation(gT[:, c, :], G[2 + c][:], ACT.Copy).then_inc(s_gts, 1)
                    if u == at["conv"] and front:
                        conv_first(A)
                    if u == at["x1"] and back:
                        act.wait_ge(s_x1t, F + 1)
                        nc.scalar.activation(x1T[:, 0, 0, :], G[1][:], ACT.Copy).then_inc(s_x1h, 1)
                    if u == at["silu"]:
                        if front:
                            silu_conv(A, 1 - par)
                        if back:
                            silu_gate(F, 0)
                            silu_gate(F, 1)
                        if front:
                            silu_z(A, 1 - par)
                        if back:
                            silu_gate(F, 2)
                            silu_gate(F, 3)
                        if front:
                            act.preload_act_table_set("natural_log_exp_and_others")
                    if back:
                        for m in due(at["hid"], u):
                            act.wait_ge(s_hid, 4 * F + 1 + m)
                            nc.scalar.activation(hid[:, 0, m, :], full[:, m, :], ACT.Copy).then_inc(s_hh, 1)
                    if u == at["b_rows"] and front:
                        copy_B(A, 1 - par)
                    if u == at["soft"] and front:
                        softplus_pre(A)
                    if u == at["ln"] and front:
                        softplus_ln(A)
                    if back:
                        gelu(g1, 2, s_h1, s_g1h, s_g1f, F, due(at["gelu1"], u))
                        gelu(g2, 3, s_h2, s_g2h, s_g2f, F, due(at["gelu2"], u))

            rounds(act, run)

        @block.vector
        def _(dve):
            def taps(b, step):
                s = step + 1
                k = TAPS - 1 - s
                for c in range(NC):
                    if step == 0:
                        dve.wait_ge(s_conv0, 2 * b + 1 + c)
                    else:
                        dve.wait_ge(s_tap, 6 * b + 2 * step - 1 + c)
                    acc = halves(conv[:, c, :])[:, :, s:SEQ]
                    nc.vector.scalar_tensor_tensor(out=acc, in0=halves(G[2 + c][:])[:, :, 0:SEQ - s],
                                                   scalar=chp_sb[:, c, CW + k:CW + k + 1], in1=acc,
                                                   op0=ALU.mult, op1=ALU.add).then_inc(s_tap, 1)

            def split_cdt(b, par):
                dve.wait_ge(s_pr, b + 1)
                nc.vector.tensor_copy(cdt[0:2 * LO, par, :], G[0][0:2 * LO, :]).then_inc(s_cdt, 1)
                dve.wait_ge(s_cdt, 2 * b + 1)
                lower = cdt[LO:2 * LO, par, :]
                nc.vector.tensor_tensor(lower, G[0][LO:2 * LO, :], lower.bitcast(F32),
                                        ALU.subtract).then_inc(s_cdt, 1)

            def stats(r, st, mv, ve, s_r, s_l, b):
                dve.wait_ge(s_r, b + 1)
                for t in range(NT):
                    last = nc.vector.bn_stats(st[:, t, :], r[:, t, :])
                last.then_inc(s_l, 1)
                dve.wait_ge(s_l, 3 * b + 1)
                nc.vector.memset(taker[:], 0.0)
                for t in range(NT):
                    last = nc.vector.bn_aggr(mv[:, t, :], st[:, t, :])
                last.then_inc(s_l, 1)
                dve.wait_ge(s_l, 3 * b + 2)
                nc.vector.tensor_scalar(ve[:], mv[:, :, 1], EPS, None, ALU.add).then_inc(s_l, 1)

            def normalise(o, r, mv, rs, s_rs, s_o, b):
                dve.wait_ge(s_rs, b + 1)
                for t in range(NT):
                    last = nc.vector.tensor_scalar(o[:, t, :], r[:, t, :], mv[:, t, 0:1], rs[:, t:t + 1],
                                                   ALU.subtract, ALU.mult)
                last.then_inc(s_o, 1)

            def split_weights(hl, src, n):
                nc.vector.tensor_copy(hl[:, 0], src).then_inc(s_wsplit, 1)
                dve.wait_ge(s_wsplit, 2 * n + 1)
                nc.vector.tensor_tensor(hl[:, 1], src, hl[:, 0].bitcast(F32), ALU.subtract).then_inc(s_wsplit, 1)

            def column(k):
                return ident[:, k:k + SELS].unsqueeze(2).to_broadcast([P, SELS, P])

            nc.vector.memset(flat(dA[:]), 0.0)
            nc.vector.memset(flat(cdt[:].bitcast(F32)), 0.0).then_inc(s_const, 1)
            dve.wait_ge(s_first, 16 * 3)
            for step in range(3):
                taps(0, step)
            nc.vector.tensor_tensor(sel[:], column(0), column(LO), ALU.add).then_inc(s_const, 1)
            for c in range(NC):
                nc.vector.tensor_scalar(diagD[:, c, :], ident[:], chp_sb[:, c, DP:DP + 1], None,
                                        ALU.mult).then_inc(s_const, 1)
            split_cdt(0, 0)
            dve.wait_ge(s_stage, 16)
            split_weights(h1_hl, full[:], 0)
            dve.wait_ge(s_stage, 16 * 2)
            split_weights(h2_hl, full[:], 1)
            dve.wait_ge(s_stage, 16 * 5)
            dve.wait_ge(s_proj, 16 * 9)
            split_weights(w1_hl, full[:, 0:1, :], 2)
            split_weights(w2_hl, full[:, 1:2, :], 3)
            w3_full = full[:, 2, :].rearrange("p (c m) -> p c m", c=NH)
            nc.vector.tensor_tensor(w3_full, w3_full, w3s_sb[:].unsqueeze(1).to_broadcast([P, NH, DM]),
                                    ALU.mult).then_inc(s_w3s, 1)
            dve.wait_ge(s_w3s, 1)
            split_weights(w3_hl, w3_full, 4)

            def run(j, par, scan, front, back, tail):
                first = isinstance(j, int) and j == 0
                F, A, T = j - 1, j + 1, j - 2
                at = DVE_AT
                for u in range(UNITS + 1):
                    if u < UNITS and scan:
                        dve.wait_ge(s_dA, UNITS * j + u + 1)
                        dve.wait_ge(s_u, UNITS * j + u + 1)
                        nc.vector.tensor_tensor_scan(hb[:, u % RING, :], dA[:, u % RING, :], ub[:, u % RING, :],
                                                     0.0, ALU.mult, ALU.add).then_inc(s_h, 1)
                    if u >= 1 and scan:
                        v = u - 1
                        n, c = divmod(v, NC)
                        dve.wait_ge(s_h, UNITS * j + v + 1)
                        if c == 0:
                            dve.wait_ge(s_cb, NS * j + n + 1)
                        if v >= OUTS or not first:
                            dve.wait_ge(s_y, UNITS * j + v - OUTS + 1)
                        nc.vector.tensor_tensor(pb[:, v % OUTS, :], hb[:, v % RING, :], CB_[n % 2][:],
                                                ALU.mult).then_inc(s_p, 1)
                    if u == at["r2"] and tail:
                        dve.wait_ge(s_w3, T + 1)
                        if not (isinstance(T, int) and T == 0):
                            dve.wait_ge(s_out, 16 * T)
                        nc.vector.tensor_tensor(flat(r2[:]), G[2][:], flat(x1[:]), ALU.add).then_inc(s_r2, 1)
                    if u == at["gate"] and back:
                        dve.wait_ge(s_y, UNITS * j)
                        dve.wait_ge(s_zs, 2 * F + 2)
                        for i in range(2):
                            nc.vector.tensor_tensor(gy[:, 2 * i:2 * i + 2, :], Y[i][:],
                                                    zs[:, 1 - par, 2 * i:2 * i + 2, :], ALU.mult).then_inc(s_gy, 1)
                    if u == at["r1"] and back:
                        dve.wait_ge(s_op, F + 1)
                        dve.wait_ge(s_xtok, 16 * F + 16)
                        nc.vector.tensor_tensor(flat(r1[:]), G[0][:], flat(xtok_sb[:]),
                                                ALU.add).then_inc(s_r1, 1)
                        stats(r1, st1, mv1, ve1, s_r1, s_l1, F)
                    if front:
                        for step in due(at["taps"], u):
                            taps(A, step)
                    if u == at["x1"] and back:
                        normalise(x1, r1, mv1, rs1, s_rs1, s_x1, F)
                    if u == at["x1_low"] and back:
                        dve.wait_ge(s_x1h, F + 1)
                        nc.vector.tensor_tensor(x1T[:, 1, 0, :], G[1][:], x1T[:, 0, 0, :].bitcast(F32),
                                                ALU.subtract).then_inc(s_x1l, 1)
                    if back:
                        for m in due(at["hid"], u):
                            dve.wait_ge(s_up, 4 * F + 1 + m)
                            dve.wait_ge(s_sg, 4 * F + 1 + m)
                            nc.vector.scalar_tensor_tensor(out=full[:, m, :], in0=G[2 + m % 2][:],
                                                           scalar=sc_sb[:, 1, m:m + 1], in1=full[:, m, :],
                                                           op0=ALU.mult, op1=ALU.mult).then_inc(s_hid, 1)
                    if u == at["cdt"] and front:
                        split_cdt(A, 1 - par)
                    if u == at["stats2"] and tail:
                        stats(r2, st2, mv2, ve2, s_r2, s_l2, T)
                    if u == at["yo"] and tail:
                        normalise(yo, r2, mv2, rs2, s_rs2, s_yo, T)
                    if back:
                        for m in due(at["g2"], u):
                            dve.wait_ge(s_g2f, 4 * F + 1 + m)
                            nc.vector.tensor_tensor(g2[:, 1, m, :], full[:, m, :], g2[:, 0, m, :].bitcast(F32),
                                                    ALU.subtract).then_inc(s_g2l, 1)

            rounds(dve, run)

        @block.tensor
        def _(pe):
            def tile_of(x, t):
                return x[:, t * P:(t + 1) * P]

            def z_proj(b, par, i):
                pe.wait_ge(s_xT, 16 * b + 16)
                for t in range(2):
                    last = nc.tensor.matmul(G[i][:, t * DI:(t + 1) * DI],
                                            tile_of(xT_sb, 2 * i + t), win_sb[:, DI:2 * DI],
                                            start=(t == 0), stop=True, skip_group_check=True)
                last.then_inc(s_z, 1)

            def in_proj(b, par, c):
                nc.tensor.matmul(G[2 + c][:], win_sb[:, c * P:(c + 1) * P], xT_sb[:],
                                 start=True, stop=True).then_inc(s_ip, 1)

            def bcdt_proj(b, par):
                for c in range(NC):
                    pe.wait_ge(s_xs, 2 * b + 1 + c)
                    last = nc.tensor.matmul(G[0][:], wpr[:, c, :], xs[:, c, :], start=(c == 0), stop=(c == NC - 1))
                last.then_inc(s_pr, 1)

            def dt_broadcast(b, par):
                pe.wait_ge(s_cdt, 2 * b + 2)
                pe.wait_ge(s_brow, b + 1)
                nc.tensor.matmul(G[0][:], sel[:BROW, NS, :], cdt[:BROW, par, :], start=True, stop=True).then_inc(s_dtb, 1)

            def c_broadcast(b, par, n, first):
                if n >= 2 or not first:
                    pe.wait_ge(s_p, UNITS * b + NC * (n - 1))
                nc.tensor.matmul(CB_[n % 2][:], sel[:BROW, n, :], cdt[:BROW, par, :], start=True, stop=True).then_inc(s_cb, 1)

            def times_high(to, w, m, k, x, start):
                nc.tensor.matmul(to, w[:, 0, k, m * P:(m + 1) * P], x[:, 0, k, :], start=start, stop=False)
                nc.tensor.matmul(to, w[:, 1, k, m * P:(m + 1) * P], x[:, 0, k, :], start=False, stop=False)

            def times_low(to, w, m, k, x, stop):
                return nc.tensor.matmul(to, w[:, 0, k, m * P:(m + 1) * P], x[:, 1, k, :], start=False, stop=stop)

            def ffn_in(to, w, m):
                times_high(to[:], w, m, 0, x1T, True)
                return times_low(to[:], w, m, 0, x1T, True)

            def hidden(w, m, part, x, s_high, s_low, s_done, b):
                for k in range(NH):
                    if part == 0:
                        if m == 0:
                            pe.wait_ge(s_high, 4 * b + 1 + k)
                        times_high(bank(m)[:], w, m, k, x, k == 0)
                    else:
                        if m == 0:
                            pe.wait_ge(s_low, 4 * b + 1 + k)
                        last = times_low(bank(m)[:], w, m, k, x, k == NH - 1)
                if part == 1:
                    last.then_inc(s_done, 1)

            pe.wait_ge(s_first, 16 * 3)
            pe.wait_ge(s_xT, 16)
            for c in range(NC):
                in_proj(0, 0, c)
            for i in range(2):
                z_proj(0, 0, i)
            pe.wait_ge(s_proj, 16 * 9)
            pe.wait_ge(s_zc, 1)
            bcdt_proj(0, 0)
            pe.wait_ge(s_const, 2 + NC)
            dt_broadcast(0, 0)
            c_broadcast(0, 0, 0, True)

            def run(j, par, scan, front, back, tail):
                first = isinstance(j, int) and j == 0
                F, A, T = j - 1, j + 1, j - 2
                at = PE_AT
                if isinstance(j, int) and j == 1:
                    pe.wait_ge(s_wsplit, 10)
                for u in range(UNITS + SUM_LAG):
                    if u >= SUM_LAG and scan:
                        v = u - SUM_LAG
                        c = v % NC
                        pe.wait_ge(s_p, UNITS * j + v + 1)
                        for t in range(NT):
                            last = nc.tensor.matmul(Y[t // 2][:, t % 2, c * P:(c + 1) * P],
                                                    tile_of(pb[:, v % OUTS, :], t), ident[:], is_transpose=True,
                                                    start=False, stop=(v >= UNITS - NC), skip_group_check=True)
                        last.then_inc(s_y, 1)
                    if u % 2 == 1 and u < UNITS - 1 and scan:
                        c_broadcast(j, par, (u + 1) // 2, first)
                    if u == UNITS - 1 and front:
                        c_broadcast(A, 1 - par, 0, False)
                    for i in due(at["z"], u) if front else ():
                        if tail:
                            pe.wait_ge(s_g2f, 4 * T + 4)
                        else:
                            pe.wait_ge(s_pre, 4 * j + 4)
                            pe.wait_ge(s_zc, 2 * j + 2)
                        z_proj(A, 1 - par, i)
                    if u == at["turn_y"] and back:
                        if tail:
                            pe.wait_ge(s_r2, T + 1)
                            pe.wait_ge(s_g2f, 4 * T + 3)
                        else:
                            pe.wait_ge(s_tap, 6 * j + 6)
                        for c in range(NC):
                            for t in range(NT):
                                pe.wait_ge(s_gy, 2 * F + 1 + t // 2)
                                last = nc.tensor.transpose(tile_of(G[2 + c], t),
                                                           gy[:, t, c * P:(c + 1) * P], ident[:])
                            last.then_inc(s_gt, 1)
                    if scan:
                        for i in due(at["start_y"], u):
                            for t in range(2):
                                for c in range(NC):
                                    nc.tensor.matmul(Y[i][:, t, c * P:(c + 1) * P],
                                                     tile_of(xs[:, c, :], 2 * i + t), diagD[:, c, :],
                                                     start=(t == 0 and c == 0), stop=False, skip_group_check=True)
                    if u == at["out_proj"] and back:
                        if front:
                            pe.wait_ge(s_zc, 2 * A + 1)
                        else:
                            pe.wait_ge(s_g2f, 4 * T + 4)
                        pe.wait_ge(s_gts, 2 * F + 2)
                        for t in range(NT):
                            for c in range(NC):
                                last = nc.tensor.matmul(tile_of(G[0], t), tile_of(gT[:, c, :], t),
                                                        wout_sb[:, c, :], start=(t == 0 and c == 0),
                                                        stop=(c == NC - 1), skip_group_check=True)
                        last.then_inc(s_op, 1)
                    for c in due(at["in_proj"], u) if front else ():
                        if back:
                            pe.wait_ge(s_gts, 2 * F + 2)
                        else:
                            pe.wait_ge(s_tap, 6 * j + 6)
                        in_proj(A, 1 - par, c)
                    if u == at["turn_x1"] and back:
                        if front:
                            pe.wait_ge(s_zc, 2 * A + 2)
                        pe.wait_ge(s_x1, F + 1)
                        for t in range(NT):
                            last = nc.tensor.transpose(tile_of(G[1], t), x1[:, t, :], ident[:])
                        last.then_inc(s_x1t, 1)
                    for part in due(at["gate_up"], u) if back else ():
                        if part == 0:
                            pe.wait_ge(s_r1, F + 1)
                            pe.wait_ge(s_x1l, F + 1)
                            if front:
                                pe.wait_ge(s_tap, 6 * A + 6)
                            ffn_in(G[0], w1_hl, 0).then_inc(s_ga, 1)
                            ffn_in(G[1], w1_hl, 1).then_inc(s_ga, 1)
                        if part == 1:
                            ffn_in(G[2], w2_hl, 0).then_inc(s_up, 1)
                            ffn_in(G[3], w2_hl, 1).then_inc(s_up, 1)
                        if part == 2:
                            for m in (2, 3):
                                pe.wait_ge(s_sg, 4 * F + m - 1)
                                ffn_in(G[m % 2], w1_hl, m).then_inc(s_ga, 1)
                        if part == 3:
                            for m in (2, 3):
                                pe.wait_ge(s_hid, 4 * F + m - 1)
                                ffn_in(G[2 + m % 2], w2_hl, m).then_inc(s_up, 1)
                    if u == at["bcdt"] and front:
                        if back:
                            pe.wait_ge(s_sg, 4 * F + 3)
                        else:
                            pe.wait_ge(s_zc, 2 * A + 1)
                        bcdt_proj(A, 1 - par)
                    if u == at["dt_row"] and front:
                        dt_broadcast(A, 1 - par)
                    for m, part in (divmod(i, 2) for i in due(at["h1"], u)) if back else ():
                        if part == 0:
                            if m == 0:
                                pe.wait_ge(s_sg, 4 * F + 4)
                            elif m < 3:
                                pe.wait_ge(s_hid, 4 * F + 2 + m)
                            elif front:
                                pe.wait_ge(s_pre, 4 * A + 4)
                        hidden(h1_hl, m, part, hid, s_hh, s_hl, s_h1, F)
                    for m, part in (divmod(i, 2) for i in due(at["h2"], u)) if back else ():
                        if part == 0:
                            pe.wait_ge(s_g1f, 4 * F + 1 + m)
                        hidden(h2_hl, m, part, g1, s_g1h, s_g1l, s_h2, F)
                    for part in due(at["w3"], u) if back else ():
                        if part == 0:
                            pe.wait_ge(s_g2f, 4 * F + 2)
                        for k in range(NH):
                            pe.wait_ge((s_g2h, s_g2l)[part], 4 * F + 1 + k)
                            for t in range(NT):
                                x = tile_of(g2[:, part, k, :], t)
                                last = nc.tensor.matmul(tile_of(G[2], t), x, w3_hl[:, 0, k, :],
                                                        start=(part == 0 and k == 0 and t == 0),
                                                        stop=(part == 1 and k == NH - 1), skip_group_check=True)
                                if part == 0:
                                    nc.tensor.matmul(tile_of(G[2], t), x, w3_hl[:, 1, k, :],
                                                     start=False, stop=False, skip_group_check=True)
                        if part == 1:
                            last.then_inc(s_w3, 1)

            rounds(pe, run)


def kernel(L0_attn_x, L0_attn_W_in, L0_attn_conv_w, L0_attn_conv_b, L0_attn_W_x, L0_attn_A_log, L0_attn_D_param,
           L0_attn_W_dt, L0_attn_b_dt, L0_attn_W_out, L0_ffn_w1_w, L0_ffn_w1_s, L0_ffn_w2_w, L0_ffn_w2_s,
           L0_ffn_h1_w, L0_ffn_h1_s, L0_ffn_h2_w, L0_ffn_h2_s, L0_ffn_w3_w, L0_ffn_w3_s):
    import concourse.bacc as _bacc
    from concourse.bass_utils import run_bass_kernel_spmd as _run

    def arr(a):
        return np.asarray(a)

    def chan(a, k):
        return arr(a).reshape(NC, P, k).transpose(1, 0, 2)

    x = arr(L0_attn_x).reshape(SEQS * SEQ, DM)
    chp = np.concatenate([chan(L0_attn_conv_w, TAPS), chan(L0_attn_conv_b, 1), chan(L0_attn_A_log, NS),
                          chan(L0_attn_D_param, 1), chan(L0_attn_W_dt, 1), chan(L0_attn_b_dt, 1)], axis=2)
    scales = np.stack([arr(s).reshape(NH, P).T for s in (L0_ffn_w1_s, L0_ffn_w2_s, L0_ffn_h1_s, L0_ffn_h2_s)], axis=1)
    ins = {
        "xT": x.T, "xtok": x, "win": arr(L0_attn_W_in).T, "wx": arr(L0_attn_W_x).T, "chp": chp,
        "wout": arr(L0_attn_W_out).T, "w1": arr(L0_ffn_w1_w).T, "w2": arr(L0_ffn_w2_w).T,
        "h1": arr(L0_ffn_h1_w).T, "h2": arr(L0_ffn_h2_w).T, "w3": arr(L0_ffn_w3_w).T, "scales": scales,
        "w3s": arr(L0_ffn_w3_s).reshape(1, DM), "ident_in": np.eye(P, dtype=np.float32),
    }
    nc = _bacc.Bacc("TRN2", target_bir_lowering=False, num_devices=1)
    arrays, args = {}, {}
    for name, a in ins.items():
        arrays[f"{name}_d"] = np.ascontiguousarray(a)
        args[name] = nc.dram_tensor(f"{name}_d", list(a.shape), mybir.dt.from_np(arrays[f"{name}_d"].dtype),
                                    kind="ExternalInput").ap()
    args["out"] = nc.dram_tensor("out_d", [SEQS * SEQ, DM], F32, kind="ExternalOutput").ap()
    build(nc, **args)
    r = _run(nc, [arrays], core_ids=[0])
    return r.results[0]["out_d"].reshape(SEQS, SEQ, DM)
```

```python
from contextlib import ExitStack

import numpy as np
import concourse.bass as bass
from concourse import mybir

F32 = mybir.dt.float32
F32R = mybir.dt.float32r
ALU = mybir.AluOpType
ACT = mybir.ActivationFunctionType

P = 128
SEQS, SEQ, DM = 32, 256, 128
DI, NS, TAPS = 256, 16, 4
NC = DI // P
HID = 512
NH = HID // P
TB = 512
NT = TB // P
PER = TB // SEQ
NB = SEQS * SEQ // TB
UNITS = NS * NC
RING = 8
OUTS = 4
QN = 4
NQ = NS // QN
SELS = NS + 1
LO = 32
BROW = 64
EPS = 1e-5
PE_AT = dict(z=(1, 5), turn_y=2, start_y=(2, 2), out_proj=3, in_proj=(3, 3), turn_x1=5, gate_up=(8, 8, 8, 10),
             bcdt=10, dt_row=12, h1=(14, 14, 15, 16, 17, 19, 21, 22), h2=(22, 23, 26, 26, 26, 27, 29, 29), w3=(2, 2))
ACT_AT = dict(z=(1, 4), y=(0, 0), conv=(2, 3), x1=10, silu=11, b_rows=14, soft=(15, 16), ln=16,
              gelu1=(16, 16, 21, 21), gelu2=(27, 27, 31, 31))
DVE_AT = dict(r2=4, gate=0, r1=5, stats1=5, taps=(5, 5, 5, 5, 5, 5), x1=5, x1_low=7, hid=(10, 10, 12, 13), cdt=12,
              xdt=25, stats2=21, yo=23)
POOL_AT = dict(rs1=3, hid=(10, 13, 13, 13), dt=21, rs2=20, g1=(17, 19, 20, 20), g2=(27, 28, 30, 30))
ACT_AHEAD, POOL_AHEAD = 4, 2
SUM_LAG = 3
CW, CB, AL, DP, WD, BD = 0, 4, 5, 21, 22, 23
CHP = 24


def build(nc, xT, xtok, win, wx, chp, wout, w1, w2, h1, h2, w3, scales, w3s, ident_in, out):
    with ExitStack() as ctx:
        def sb(name, shape, dt=F32):
            return ctx.enter_context(nc.sbuf_tensor(name, shape, dt))

        def sem(name):
            return ctx.enter_context(nc.semaphore(name))

        win_sb = sb("win_sb", [P, 2 * DI])
        wpr = sb("wpr", [P, NC, P])
        wout_sb = sb("wout_sb", [P, NC, DM])
        w1_hl = sb("w1_hl", [P, 2, 1, HID], F32R)
        w2_hl = sb("w2_hl", [P, 2, 1, HID], F32R)
        h1_hl = sb("h1_hl", [P, 2, NH, HID], F32R)
        h2_hl = sb("h2_hl", [P, 2, NH, HID], F32R)
        w3_hl = sb("w3_hl", [P, 2, NH, DM], F32R)
        w3s_sb = sb("w3s_sb", [P, DM])
        chp_sb = sb("chp_sb", [P, NC, CHP])
        sc_sb = sb("sc_sb", [P, 4, NH])
        negA = sb("negA", [P, NC, NS])
        ident = sb("ident", [P, P])
        diagD = sb("diagD", [P, NC, P])
        sel = sb("sel", [P, SELS, P], F32R)
        mhalf = sb("mhalf", [P, NT])
        xT_sb = sb("xT_sb", [P, TB])
        xtok_sb = sb("xtok_sb", [P, NT, DM])
        conv = sb("conv", [P, NC, TB])
        xs = sb("xs", [P, NC, TB])
        zs = sb("zs", [P, 2, NT, DI])
        cdt = sb("cdt", [P, 2, TB], F32R)
        soft = conv
        dt = sb("dt", [P, 2, NC, TB])
        xdt = sb("xdt", [P, 2, NC, TB])
        brow = xdt[BROW:BROW + NS, :, NC - 1, :]
        bbc = sb("bbc", [P, 2, QN, TB])
        dA = sb("dA", [P, RING, TB])
        ub = sb("ub", [P, RING, TB])
        hb = ub
        pb = sb("pb", [P, OUTS, TB])
        gy = sb("gy", [P, NT, DI])
        gT = conv
        r1 = sb("r1", [P, NT, DM])
        x1 = r1
        relu = gy[:].rearrange("p t d -> p (t d)").rearrange("p (c t) -> p c t", c=NC)
        x1T = sb("x1T", [P, 2, 1, TB], F32R)
        hid = sb("hid", [P, 2, NH, TB], F32R)
        g1 = sb("g1", [P, 2, NH, TB], F32R)
        g2 = hid
        full = sb("full", [P, NH, TB])
        r2 = sb("r2", [P, NT, DM])
        yo = r2
        st1, mv1, ve1, rs1 = sb("st1", [P, NT, 6]), sb("mv1", [P, NT, 2]), sb("ve1", [P, NT]), sb("rs1", [P, NT])
        st2, mv2, ve2, rs2 = sb("st2", [P, NT, 6]), sb("mv2", [P, NT, 2]), sb("ve2", [P, NT]), sb("rs2", [P, NT])
        taker = sb("taker", [P, 1])
        bscr = nc.dram_tensor("bscr", [2, NS * TB], F32, kind="Internal").ap()

        G = [ctx.enter_context(nc.psum_tensor(f"G{i}", [P, TB], F32)) for i in range(4)]
        Y = [ctx.enter_context(nc.psum_tensor(f"Y{i}", [P, 2, DI], F32)) for i in range(2)]
        CB_ = [ctx.enter_context(nc.psum_tensor(f"C{i}", [P, TB], F32)) for i in range(2)]

        s_first, s_proj = sem("s_first"), sem("s_proj")
        s_stage = [sem("s_stage_h1"), sem("s_stage_h2"), sem("s_stage_w")]
        s_zero, s_const, s_aexp, s_aneg = sem("s_zero"), sem("s_const"), sem("s_aexp"), sem("s_aneg")
        s_w3s = sem("s_w3s")
        s_wsplit = sem("s_wsplit")
        s_wh1, s_wl1 = sem("s_wh1"), sem("s_wl1")
        s_xT = sem("s_xT")
        s_xtok = sem("s_xtok")
        s_z = sem("s_z")
        s_zc = sem("s_zc")
        s_zs = sem("s_zs")
        s_ip = sem("s_ip")
        s_conv0 = sem("s_conv0")
        s_tap = sem("s_tap")
        s_xs = sem("s_xs")
        s_pr = sem("s_pr")
        s_cdt = sem("s_cdt")
        s_brow = sem("s_brow")
        s_bst = sem("s_bst")
        s_bbc = [sem(f"s_bbc{q}") for q in range(NQ)]
        s_dtb = sem("s_dtb")
        s_pre = sem("s_pre")
        s_soft = sem("s_soft")
        s_dt = sem("s_dt")
        s_xdt = sem("s_xdt")
        s_dA = sem("s_dA")
        s_u = sem("s_u")
        s_h = sem("s_h")
        s_cb = sem("s_cb")
        s_p = sem("s_p")
        s_y = sem("s_y")
        s_gy = sem("s_gy")
        s_gt = sem("s_gt")
        s_gts = sem("s_gts")
        s_op = sem("s_op")
        s_r1 = sem("s_r1")
        s_l1 = sem("s_l1")
        s_rs1 = sem("s_rs1")
        s_x1 = sem("s_x1")
        s_x1t = sem("s_x1t")
        s_x1h, s_x1l = sem("s_x1h"), sem("s_x1l")
        s_ga, s_sg = sem("s_ga"), sem("s_sg")
        s_up, s_hid = sem("s_up"), sem("s_hid")
        s_hh, s_hl = sem("s_hh"), sem("s_hl")
        s_h1 = sem("s_h1")
        s_g1h, s_g1f, s_g1l = sem("s_g1h"), sem("s_g1f"), sem("s_g1l")
        s_h2 = sem("s_h2")
        s_g2h, s_g2f, s_g2l = sem("s_g2h"), sem("s_g2f"), sem("s_g2l")
        s_w3 = sem("s_w3")
        s_r2 = sem("s_r2")
        s_l2, s_rs2, s_yo = sem("s_l2"), sem("s_rs2"), sem("s_yo")
        s_out = sem("s_out")

        def halves(x):
            return x.rearrange("p (s t) -> p s t", s=PER)

        def flat(x):
            return x.rearrange("p a b -> p (a b)")

        def due(slots, u):
            return [i for i, slot in enumerate(slots) if slot == u]

        BZ = (G[0], G[1])
        BTURN = (G[2], G[3])
        BOUT = G[2]
        BIN = (G[3], G[0])
        BX1 = G[1]
        BGATE, BUP = (G[2], G[1]), (G[3], G[0])
        BPR = G[2]
        BHID = (G[1], G[3], G[0], G[2])
        BW3 = G[1]

        def rounds(eng, run):
            run(0, 0, True, True, False, False)
            run(1, 1, True, True, True, False)
            with eng.Fori(0, (NB - 4) // 2) as i:
                run(i * 2 + 2, 0, True, True, True, True)
                run(i * 2 + 3, 1, True, True, True, True)
            run(NB - 2, 0, True, True, True, True)
            run(NB - 1, 1, True, False, True, True)
            run(NB, 0, False, False, True, True)
            run(NB + 1, 1, False, False, False, True)

        block = ctx.enter_context(nc.Block())

        @block.sync
        def _(sp):
            def load_xT(b):
                sp.dma_start(xT_sb[:], xT[:, bass.ts(b, TB)]).then_inc(s_xT, 16)

            def store_B(b, par):
                sp.wait_ge(s_brow, b + 1)
                sp.dma_start(bscr[par].rearrange("(n t) -> n t", n=NS), brow[:, par, :]).then_inc(s_bst, 16)

            def broadcast_B(b, par, q, free):
                if free is not None:
                    sp.wait_ge(s_u, free)
                if q == 0:
                    sp.wait_ge(s_bst, 16 * b + 16)
                piece = bscr[par:par + 1, q * QN * TB:(q + 1) * QN * TB]
                sp.dma_start(flat(bbc[:, q % 2, :, :]), piece.to_broadcast([P, QN * TB])).then_inc(s_bbc[q], 16)

            load_xT(0)
            sp.dma_start(win_sb[:], win).then_inc(s_first, 16)
            sp.dma_start(chp_sb[:], chp).then_inc(s_first, 16)
            sp.dma_start(ident[:], ident_in).then_inc(s_first, 16)
            sp.wait_ge(s_zero, 2)
            for c in range(NC):
                rows = wx[c * P:(c + 1) * P, :]
                for at, lo, hi in ((0, NS, 2 * NS + 1), (LO, NS, 2 * NS + 1), (BROW, 0, NS)):
                    sp.dma_start(wpr[:, c, at:at + hi - lo], rows[:, lo:hi]).then_inc(s_proj, 16)
            sp.dma_start(wout_sb[:], wout.rearrange("(c p) m -> p c m", p=P)).then_inc(s_proj, 16)
            sp.dma_start(sc_sb[:], scales).then_inc(s_proj, 16)
            sp.dma_start(w3s_sb[:], w3s.to_broadcast([P, DM])).then_inc(s_proj, 16)
            sp.dma_start(ub[:, 0:NH, :], h1.rearrange("(c p) m -> p c m", p=P)).then_inc(s_stage[0], 16)
            sp.dma_start(ub[:, NH:2 * NH, :], h2.rearrange("(c p) m -> p c m", p=P)).then_inc(s_stage[1], 16)
            sp.dma_start(full[:, 0, :], w1).then_inc(s_stage[2], 16)
            sp.dma_start(full[:, 1, :], w2).then_inc(s_stage[2], 16)
            sp.dma_start(full[:, 2, :].rearrange("p (c m) -> p c m", c=NH),
                         w3.rearrange("(c p) m -> p c m", p=P)).then_inc(s_stage[2], 16)
            sp.wait_ge(s_ip, 2)
            sp.wait_ge(s_z, 2)
            load_xT(1)
            store_B(0, 0)
            broadcast_B(0, 0, 0, None)
            broadcast_B(0, 0, 1, None)

            def run(j, par, scan, front, back, tail):
                F, A, T = j - 1, j + 1, j - 2
                if front and not (isinstance(j, int) and j + 2 >= NB):
                    sp.wait_ge(s_ip, 2 * A + 2)
                    sp.wait_ge(s_z, 2 * A + 2)
                    load_xT(j + 2)
                if scan:
                    if back:
                        sp.wait_ge(s_r1, F + 1)
                    sp.dma_start(xtok_sb[:], xtok[bass.ts(j, TB), :].rearrange("(t p) m -> p t m", p=P)).then_inc(s_xtok, 16)
                    broadcast_B(j, par, 2, NS * j + QN)
                if front:
                    store_B(A, 1 - par)
                if scan:
                    broadcast_B(j, par, 3, NS * j + 2 * QN)
                if front:
                    broadcast_B(A, 1 - par, 0, NS * j + 3 * QN)
                if tail:
                    sp.wait_ge(s_yo, T + 1)
                    sp.dma_start(out[bass.ts(T, TB), :].rearrange("(t p) m -> p t m", p=P),
                                 yo[:]).then_inc(s_out, 16)
                if front:
                    broadcast_B(A, 1 - par, 1, NS * j + 4 * QN)

            rounds(sp, run)
            sp.wait_ge(s_out, 16 * NB)

        @block.gpsimd
        def _(pool):
            def add_dt(b, par):
                pool.wait_ge(s_soft, 2 * b + 2)
                nc.gpsimd.tensor_tensor(dt[:, par, :, :], relu, soft[:], ALU.add).then_inc(s_dt, 1)

            def input_term(b, par, n, first):
                u = NC * n
                if n == 0:
                    pool.wait_ge(s_xdt, b + 1)
                if n % QN == 0:
                    pool.wait_ge(s_bbc[n // QN], 16 * b + 16)
                if u >= RING or not first:
                    pool.wait_ge(s_p, UNITS * b + u - RING + NC)
                bn = bbc[:, n // QN % 2, n % QN, :].unsqueeze(1).to_broadcast([P, NC, TB])
                nc.gpsimd.tensor_tensor(ub[:, u % RING:u % RING + NC, :], xdt[:, par, :, :], bn,
                                        ALU.mult).then_inc(s_u, 1)

            def low(x, m, s_full, s_low, b):
                pool.wait_ge(s_full, 4 * b + 1 + m)
                nc.gpsimd.tensor_tensor(x[:, 1, m, :], full[:, m, :], x[:, 0, m, :].bitcast(F32),
                                        ALU.subtract).then_inc(s_low, 1)

            nc.gpsimd.memset(mhalf[:], -0.5).then_inc(s_zero, 1)
            nc.gpsimd.memset(flat(wpr[:]), 0.0).then_inc(s_zero, 1)
            pool.wait_ge(s_wh1, 1)
            nc.gpsimd.tensor_tensor(h1_hl[:, 1], ub[:, 0:NH, :], h1_hl[:, 0].bitcast(F32),
                                    ALU.subtract).then_inc(s_wl1, 1)
            add_dt(0, 0)
            pool.wait_ge(s_wl1, 1)
            pool.wait_ge(s_wsplit, 2)
            for n in range(POOL_AHEAD):
                input_term(0, 0, n, True)

            def run(j, par, scan, front, back, tail):
                first = isinstance(j, int) and j == 0
                F, A, T = j - 1, j + 1, j - 2
                at = POOL_AT
                for u in range(UNITS):
                    ahead = u // NC + POOL_AHEAD
                    if u % NC == 0 and ahead < NS and scan:
                        input_term(j, par, ahead, first)
                    if u % NC == 0 and ahead >= NS and front:
                        input_term(A, 1 - par, ahead - NS, False)
                    if u == at["rs1"] and back:
                        pool.wait_ge(s_l1, 3 * F + 3)
                        nc.gpsimd.tensor_tensor(rs1[:], ve1[:], mhalf[:], ALU.pow).then_inc(s_rs1, 1)
                    if back:
                        for m in due(at["hid"], u):
                            low(hid, m, s_hh, s_hl, F)
                    if u == at["dt"] and front:
                        add_dt(A, 1 - par)
                    if u == at["rs2"] and tail:
                        pool.wait_ge(s_l2, 3 * T + 3)
                        nc.gpsimd.tensor_tensor(rs2[:], ve2[:], mhalf[:], ALU.pow).then_inc(s_rs2, 1)
                    if back:
                        for m in due(at["g1"], u):
                            low(g1, m, s_g1f, s_g1l, F)
                        for m in due(at["g2"], u):
                            low(g2, m, s_g2f, s_g2l, F)

            rounds(pool, run)

        @block.scalar
        def _(act):
            def decay(b, par, u, first):
                n, c = divmod(u, NC)
                if u == 0:
                    act.wait_ge(s_dt, b + 1)
                if u >= RING or not first:
                    act.wait_ge(s_h, UNITS * b + u - RING + 1)
                nc.scalar.activation(halves(dA[:, u % RING, :])[:, :, 1:SEQ],
                                     halves(dt[:, par, c, :])[:, :, 1:SEQ], ACT.Exp,
                                     scale=negA[:, c, n:n + 1]).then_inc(s_dA, 1)

            def copy_z(b, par, i, back):
                if back:
                    act.wait_ge(s_gy, 2 * (b - 2) + 1 + i)
                act.wait_ge(s_z, 2 * b + 1 + i)
                nc.scalar.activation(flat(zs[:, par, 2 * i:2 * i + 2, :]), BZ[i][:], ACT.Copy).then_inc(s_zc, 1)

            def conv_first(b, c):
                act.wait_ge(s_ip, 2 * b + 1 + c)
                nc.scalar.activation(conv[:, c, :], BIN[c][:], ACT.Identity, bias=chp_sb[:, c, CB:CB + 1],
                                     scale=chp_sb[:, c, CW + TAPS - 1:CW + TAPS]).then_inc(s_conv0, 1)

            def silu_conv(b, par):
                for c in range(NC):
                    act.wait_ge(s_tap, 6 * b + 5 + c)
                    nc.scalar.activation(xs[:, c, :], conv[:, c, :], ACT.Silu).then_inc(s_xs, 1)

            def silu_z(b, par):
                act.wait_ge(s_zc, 2 * b + 2)
                for i in range(2):
                    z = flat(zs[:, par, 2 * i:2 * i + 2, :])
                    nc.scalar.activation(z, z, ACT.Silu).then_inc(s_zs, 1)

            def silu_gate(b, m):
                act.wait_ge(s_ga, 4 * b + 1 + m)
                nc.scalar.activation(full[:, m, :], BGATE[m % 2][:], ACT.Silu,
                                     scale=sc_sb[:, 0, m:m + 1]).then_inc(s_sg, 1)

            def gelu(x, kind, s_in, s_high, s_full, b, ms):
                for m in ms:
                    act.wait_ge(s_in, 4 * b + 1 + m)
                    scale = sc_sb[:, kind, m:m + 1]
                    nc.scalar.activation(x[:, 0, m, :], BHID[m][:], ACT.Gelu, scale=scale).then_inc(s_high, 1)
                    nc.scalar.activation(full[:, m, :], BHID[m][:], ACT.Gelu, scale=scale).then_inc(s_full, 1)

            def copy_B(b, par):
                act.wait_ge(s_pr, b + 1)
                nc.scalar.activation(brow[:, par, :], BPR[BROW:BROW + NS, :], ACT.Copy).then_inc(s_brow, 1)

            def softplus_pre(b, c):
                act.wait_ge(s_dtb, b + 1)
                for f, o in ((ACT.Abs, soft), (ACT.Relu, relu)):
                    nc.scalar.activation(o[:, c, :], BPR[:], f, bias=chp_sb[:, c, BD:BD + 1],
                                         scale=chp_sb[:, c, WD:WD + 1]).then_inc(s_pre, 1)

            def softplus_ln(b):
                v = flat(soft[:])
                act.wait_ge(s_pre, 4 * b + 4)
                nc.scalar.activation(v, v, ACT.Exp, scale=-1.0).then_inc(s_soft, 1)
                act.wait_ge(s_soft, 2 * b + 1)
                nc.scalar.activation(v, v, ACT.Ln, bias=1.0).then_inc(s_soft, 1)

            act.wait_ge(s_first, 16 * 3)
            for c in range(NC):
                conv_first(0, c)
            silu_conv(0, 0)
            for i in range(2):
                copy_z(0, 0, i, False)
            silu_z(0, 0)
            act.preload_act_table_set("natural_log_exp_and_others")
            copy_B(0, 0)
            for c in range(NC):
                softplus_pre(0, c)
            softplus_ln(0)
            for c in range(NC):
                nc.scalar.activation(negA[:, c, :], chp_sb[:, c, AL:AL + NS], ACT.Exp).then_inc(s_aexp, 1)
            act.wait_ge(s_aexp, NC)
            nc.scalar.mul(flat(negA[:]), flat(negA[:]), -1.0).then_inc(s_aneg, 1)
            act.wait_ge(s_aneg, 1)
            act.wait_ge(s_const, 1)
            for u in range(ACT_AHEAD):
                decay(0, 0, u, True)

            def run(j, par, scan, front, back, tail):
                first = isinstance(j, int) and j == 0
                F, A = j - 1, j + 1
                at = ACT_AT
                for u in range(UNITS):
                    ahead = u + ACT_AHEAD
                    if ahead < UNITS and scan:
                        decay(j, par, ahead, first)
                    if ahead >= UNITS and front:
                        decay(A, 1 - par, ahead - UNITS, False)
                    for c in due(at["y"], u) if back else ():
                        act.wait_ge(s_gt, 2 * F + 1 + c)
                        nc.scalar.activation(gT[:, c, :], BTURN[c][:], ACT.Copy).then_inc(s_gts, 1)
                    for i in due(at["z"], u) if front else ():
                        copy_z(A, 1 - par, i, back)
                    for c in due(at["conv"], u) if front else ():
                        conv_first(A, c)
                    if u == at["x1"] and back:
                        act.wait_ge(s_x1t, F + 1)
                        nc.scalar.activation(x1T[:, 0, 0, :], BX1[:], ACT.Copy).then_inc(s_x1h, 1)
                    if u == at["silu"]:
                        if front:
                            silu_conv(A, 1 - par)
                        if back:
                            silu_gate(F, 0)
                            silu_gate(F, 1)
                        if front:
                            silu_z(A, 1 - par)
                        if back:
                            silu_gate(F, 2)
                            silu_gate(F, 3)
                        if front:
                            act.preload_act_table_set("natural_log_exp_and_others")
                    if u == at["b_rows"] and front:
                        copy_B(A, 1 - par)
                    for c in due(at["soft"], u) if front else ():
                        softplus_pre(A, c)
                    if u == at["ln"] and front:
                        softplus_ln(A)
                    if back:
                        gelu(g1, 2, s_h1, s_g1h, s_g1f, F, due(at["gelu1"], u))
                        gelu(g2, 3, s_h2, s_g2h, s_g2f, F, due(at["gelu2"], u))

            rounds(act, run)

        @block.vector
        def _(dve):
            def tap(b, step, c):
                s = step + 1
                k = TAPS - 1 - s
                if step == 0:
                    dve.wait_ge(s_conv0, 2 * b + 1 + c)
                else:
                    dve.wait_ge(s_tap, 6 * b + 2 * step - 1 + c)
                acc = halves(conv[:, c, :])[:, :, s:SEQ]
                nc.vector.scalar_tensor_tensor(out=acc, in0=halves(BIN[c][:])[:, :, 0:SEQ - s],
                                               scalar=chp_sb[:, c, CW + k:CW + k + 1], in1=acc,
                                               op0=ALU.mult, op1=ALU.add).then_inc(s_tap, 1)

            def mult_xdt(b, par):
                dve.wait_ge(s_dt, b + 1)
                dve.wait_ge(s_xs, 2 * b + 2)
                dve.wait_ge(s_bst, 16 * b + 16)
                nc.vector.tensor_tensor(xdt[:, par, :, :], dt[:, par, :, :], xs[:], ALU.mult).then_inc(s_xdt, 1)

            def split_cdt(b, par):
                dve.wait_ge(s_pr, b + 1)
                nc.vector.tensor_copy(cdt[0:2 * LO, par, :], BPR[0:2 * LO, :]).then_inc(s_cdt, 1)
                dve.wait_ge(s_cdt, 2 * b + 1)
                lower = cdt[LO:2 * LO, par, :]
                nc.vector.tensor_tensor(lower, BPR[LO:2 * LO, :], lower.bitcast(F32),
                                        ALU.subtract).then_inc(s_cdt, 1)

            def stats(r, st, mv, ve, s_r, s_l, b):
                dve.wait_ge(s_r, b + 1)
                for t in range(NT):
                    last = nc.vector.bn_stats(st[:, t, :], r[:, t, :])
                last.then_inc(s_l, 1)
                dve.wait_ge(s_l, 3 * b + 1)
                nc.vector.memset(taker[:], 0.0)
                for t in range(NT):
                    last = nc.vector.bn_aggr(mv[:, t, :], st[:, t, :])
                last.then_inc(s_l, 1)
                dve.wait_ge(s_l, 3 * b + 2)
                nc.vector.tensor_scalar(ve[:], mv[:, :, 1], EPS, None, ALU.add).then_inc(s_l, 1)

            def normalise(o, r, mv, rs, s_rs, s_o, b):
                dve.wait_ge(s_rs, b + 1)
                for t in range(NT):
                    last = nc.vector.tensor_scalar(o[:, t, :], r[:, t, :], mv[:, t, 0:1], rs[:, t:t + 1],
                                                   ALU.subtract, ALU.mult)
                last.then_inc(s_o, 1)

            def split_weights(hl, src, n):
                nc.vector.tensor_copy(hl[:, 0], src).then_inc(s_wsplit, 1)
                dve.wait_ge(s_wsplit, 2 * n + 1)
                nc.vector.tensor_tensor(hl[:, 1], src, hl[:, 0].bitcast(F32), ALU.subtract).then_inc(s_wsplit, 1)

            def column(k):
                return ident[:, k:k + SELS].unsqueeze(2).to_broadcast([P, SELS, P])

            nc.vector.memset(flat(dA[:]), 0.0)
            nc.vector.memset(flat(cdt[:].bitcast(F32)), 0.0).then_inc(s_const, 1)
            dve.wait_ge(s_first, 16 * 3)
            for i in range(NC * (TAPS - 1)):
                tap(0, *divmod(i, NC))
            nc.vector.tensor_tensor(sel[:], column(0), column(LO), ALU.add).then_inc(s_const, 1)
            for c in range(NC):
                nc.vector.tensor_scalar(diagD[:, c, :], ident[:], chp_sb[:, c, DP:DP + 1], None,
                                        ALU.mult).then_inc(s_const, 1)
            dve.wait_ge(s_stage[0], 16)
            nc.vector.tensor_copy(h1_hl[:, 0], ub[:, 0:NH, :]).then_inc(s_wh1, 1)
            split_cdt(0, 0)
            dve.wait_ge(s_stage[1], 16)
            split_weights(h2_hl, ub[:, NH:2 * NH, :], 0)
            dve.wait_ge(s_stage[2], 16 * 3)
            dve.wait_ge(s_proj, 16 * 9)
            split_weights(w1_hl, full[:, 0:1, :], 1)
            split_weights(w2_hl, full[:, 1:2, :], 2)
            w3_full = full[:, 2, :].rearrange("p (c m) -> p c m", c=NH)
            nc.vector.tensor_tensor(w3_full, w3_full, w3s_sb[:].unsqueeze(1).to_broadcast([P, NH, DM]),
                                    ALU.mult).then_inc(s_w3s, 1)
            dve.wait_ge(s_w3s, 1)
            split_weights(w3_hl, w3_full, 3)
            mult_xdt(0, 0)

            def run(j, par, scan, front, back, tail):
                first = isinstance(j, int) and j == 0
                F, A, T = j - 1, j + 1, j - 2
                at = DVE_AT
                for u in range(UNITS + 1):
                    if u < UNITS and scan:
                        dve.wait_ge(s_dA, UNITS * j + u + 1)
                        dve.wait_ge(s_u, NS * j + u // NC + 1)
                        nc.vector.tensor_tensor_scan(hb[:, u % RING, :], dA[:, u % RING, :], ub[:, u % RING, :],
                                                     0.0, ALU.mult, ALU.add).then_inc(s_h, 1)
                    if u >= 1 and scan:
                        v = u - 1
                        n, c = divmod(v, NC)
                        dve.wait_ge(s_h, UNITS * j + v + 1)
                        if c == 0:
                            dve.wait_ge(s_cb, NS * j + n + 1)
                        if v >= OUTS or not first:
                            dve.wait_ge(s_y, UNITS * j + v - OUTS + 1)
                        nc.vector.tensor_tensor(pb[:, v % OUTS, :], hb[:, v % RING, :], CB_[n % 2][:],
                                                ALU.mult).then_inc(s_p, 1)
                    if u == at["gate"] and back:
                        dve.wait_ge(s_y, UNITS * j)
                        dve.wait_ge(s_zs, 2 * F + 2)
                        for i in range(2):
                            nc.vector.tensor_tensor(gy[:, 2 * i:2 * i + 2, :], Y[i][:],
                                                    zs[:, 1 - par, 2 * i:2 * i + 2, :], ALU.mult).then_inc(s_gy, 1)
                    if u == at["r2"] and tail:
                        dve.wait_ge(s_w3, T + 1)
                        if not (isinstance(T, int) and T == 0):
                            dve.wait_ge(s_out, 16 * T)
                        nc.vector.tensor_tensor(flat(r2[:]), BW3[:], flat(x1[:]), ALU.add).then_inc(s_r2, 1)
                    if u == at["r1"] and back:
                        if tail:
                            dve.wait_ge(s_r2, T + 1)
                        dve.wait_ge(s_op, F + 1)
                        dve.wait_ge(s_xtok, 16 * F + 16)
                        nc.vector.tensor_tensor(flat(r1[:]), BOUT[:], flat(xtok_sb[:]),
                                                ALU.add).then_inc(s_r1, 1)
                    if u == at["stats1"] and back:
                        stats(r1, st1, mv1, ve1, s_r1, s_l1, F)
                    if front:
                        for i in due(at["taps"], u):
                            tap(A, *divmod(i, NC))
                    if u == at["x1"] and back:
                        normalise(x1, r1, mv1, rs1, s_rs1, s_x1, F)
                    if u == at["x1_low"] and back:
                        dve.wait_ge(s_x1h, F + 1)
                        nc.vector.tensor_tensor(x1T[:, 1, 0, :], BX1[:], x1T[:, 0, 0, :].bitcast(F32),
                                                ALU.subtract).then_inc(s_x1l, 1)
                    if back:
                        for m in due(at["hid"], u):
                            dve.wait_ge(s_up, 4 * F + 1 + m)
                            dve.wait_ge(s_sg, 4 * F + 1 + m)
                            nc.vector.scalar_tensor_tensor(out=full[:, m, :], in0=BUP[m % 2][:],
                                                           scalar=sc_sb[:, 1, m:m + 1], in1=full[:, m, :],
                                                           op0=ALU.mult, op1=ALU.mult).then_inc(s_hid, 1)
                            dve.wait_ge(s_hid, 4 * F + 1 + m)
                            nc.vector.tensor_copy(hid[:, 0, m, :], full[:, m, :]).then_inc(s_hh, 1)
                    if u == at["cdt"] and front:
                        split_cdt(A, 1 - par)
                    if u == at["xdt"] and front:
                        mult_xdt(A, 1 - par)
                    if u == at["stats2"] and tail:
                        stats(r2, st2, mv2, ve2, s_r2, s_l2, T)
                    if u == at["yo"] and tail:
                        normalise(yo, r2, mv2, rs2, s_rs2, s_yo, T)

            rounds(dve, run)

        @block.tensor
        def _(pe):
            def tile_of(x, t):
                return x[:, t * P:(t + 1) * P]

            def z_proj(b, par, i):
                pe.wait_ge(s_xT, 16 * b + 16)
                for t in range(2):
                    last = nc.tensor.matmul(BZ[i][:, t * DI:(t + 1) * DI],
                                            tile_of(xT_sb, 2 * i + t), win_sb[:, DI:2 * DI],
                                            start=(t == 0), stop=True, skip_group_check=True)
                last.then_inc(s_z, 1)

            def in_proj(b, par, c):
                nc.tensor.matmul(BIN[c][:], win_sb[:, c * P:(c + 1) * P], xT_sb[:],
                                 start=True, stop=True).then_inc(s_ip, 1)

            def bcdt_proj(b, par):
                for c in range(NC):
                    pe.wait_ge(s_xs, 2 * b + 1 + c)
                    last = nc.tensor.matmul(BPR[:], wpr[:, c, :], xs[:, c, :], start=(c == 0), stop=(c == NC - 1))
                last.then_inc(s_pr, 1)

            def dt_broadcast(b, par):
                pe.wait_ge(s_cdt, 2 * b + 2)
                pe.wait_ge(s_brow, b + 1)
                nc.tensor.matmul(BPR[:], sel[:BROW, NS, :], cdt[:BROW, par, :], start=True, stop=True).then_inc(s_dtb, 1)

            def c_broadcast(b, par, n, first):
                if n >= 2 or not first:
                    pe.wait_ge(s_p, UNITS * b + NC * (n - 1))
                nc.tensor.matmul(CB_[n % 2][:], sel[:BROW, n, :], cdt[:BROW, par, :], start=True, stop=True).then_inc(s_cb, 1)

            def times_high(to, w, m, k, x, start):
                nc.tensor.matmul(to, w[:, 0, k, m * P:(m + 1) * P], x[:, 0, k, :], start=start, stop=False)
                nc.tensor.matmul(to, w[:, 1, k, m * P:(m + 1) * P], x[:, 0, k, :], start=False, stop=False)

            def times_low(to, w, m, k, x, stop):
                return nc.tensor.matmul(to, w[:, 0, k, m * P:(m + 1) * P], x[:, 1, k, :], start=False, stop=stop)

            def ffn_in(to, w, m):
                times_high(to[:], w, m, 0, x1T, True)
                return times_low(to[:], w, m, 0, x1T, True)

            def hidden(w, m, part, x, s_high, s_low, s_done, b):
                for k in range(NH):
                    if part == 0:
                        if m == 0:
                            pe.wait_ge(s_high, 4 * b + 1 + k)
                        times_high(BHID[m][:], w, m, k, x, k == 0)
                    else:
                        if m == 0:
                            pe.wait_ge(s_low, 4 * b + 1 + k)
                        last = times_low(BHID[m][:], w, m, k, x, k == NH - 1)
                if part == 1:
                    last.then_inc(s_done, 1)

            pe.wait_ge(s_first, 16 * 3)
            pe.wait_ge(s_xT, 16)
            for c in range(NC):
                in_proj(0, 0, c)
            pe.wait_ge(s_tap, 6)
            for i in range(2):
                z_proj(0, 0, i)
            pe.wait_ge(s_proj, 16 * 9)
            bcdt_proj(0, 0)
            pe.wait_ge(s_const, 2 + NC)
            dt_broadcast(0, 0)
            c_broadcast(0, 0, 0, True)

            def run(j, par, scan, front, back, tail):
                first = isinstance(j, int) and j == 0
                F, A, T = j - 1, j + 1, j - 2
                at = PE_AT
                if isinstance(j, int) and j == 1:
                    pe.wait_ge(s_wsplit, 8)
                    pe.wait_ge(s_wl1, 1)
                for u in range(UNITS + SUM_LAG):
                    if u >= SUM_LAG and scan:
                        v = u - SUM_LAG
                        c = v % NC
                        pe.wait_ge(s_p, UNITS * j + v + 1)
                        for t in range(NT):
                            last = nc.tensor.matmul(Y[t // 2][:, t % 2, c * P:(c + 1) * P],
                                                    tile_of(pb[:, v % OUTS, :], t), ident[:], is_transpose=True,
                                                    start=False, stop=(v >= UNITS - NC), skip_group_check=True)
                        last.then_inc(s_y, 1)
                    if u % 2 == 1 and u < UNITS - 1 and scan:
                        c_broadcast(j, par, (u + 1) // 2, first)
                    if u == UNITS - 1 and front:
                        c_broadcast(A, 1 - par, 0, False)
                    for i in due(at["z"], u) if front else ():
                        if tail:
                            if i == 0:
                                pe.wait_ge(s_g2f, 4 * T + 3)
                            else:
                                pe.wait_ge(s_r2, T + 1)
                        else:
                            pe.wait_ge(s_tap, 6 * j + 6)
                            pe.wait_ge(s_zc, 2 * j + 2)
                        z_proj(A, 1 - par, i)
                    if u == at["turn_y"] and back:
                        if tail:
                            pe.wait_ge(s_g2f, 4 * T + 4)
                        else:
                            pe.wait_ge(s_pre, 4 * j + 4)
                            pe.wait_ge(s_tap, 6 * j + 6)
                        for c in range(NC):
                            for t in range(NT):
                                pe.wait_ge(s_gy, 2 * F + 1 + t // 2)
                                last = nc.tensor.transpose(tile_of(BTURN[c], t),
                                                           gy[:, t, c * P:(c + 1) * P], ident[:])
                            last.then_inc(s_gt, 1)
                    if scan:
                        for i in due(at["start_y"], u):
                            for t in range(2):
                                for c in range(NC):
                                    nc.tensor.matmul(Y[i][:, t, c * P:(c + 1) * P],
                                                     tile_of(xs[:, c, :], 2 * i + t), diagD[:, c, :],
                                                     start=(t == 0 and c == 0), stop=False, skip_group_check=True)
                    for part in due(at["w3"], u) if tail else ():
                        if part == 0:
                            pe.wait_ge(s_g2f, 4 * T + 4)
                        for k in range(NH):
                            pe.wait_ge((s_g2h, s_g2l)[part], 4 * T + 1 + k)
                            for t in range(NT):
                                x = tile_of(g2[:, part, k, :], t)
                                last = nc.tensor.matmul(tile_of(BW3, t), x, w3_hl[:, 0, k, :],
                                                        start=(part == 0 and k == 0 and t == 0),
                                                        stop=(part == 1 and k == NH - 1), skip_group_check=True)
                                if part == 0:
                                    nc.tensor.matmul(tile_of(BW3, t), x, w3_hl[:, 1, k, :],
                                                     start=False, stop=False, skip_group_check=True)
                        if part == 1:
                            last.then_inc(s_w3, 1)
                    if u == at["out_proj"] and back:
                        pe.wait_ge(s_gts, 2 * F + 2)
                        for t in range(NT):
                            for c in range(NC):
                                last = nc.tensor.matmul(tile_of(BOUT, t), tile_of(gT[:, c, :], t),
                                                        wout_sb[:, c, :], start=(t == 0 and c == 0),
                                                        stop=(c == NC - 1), skip_group_check=True)
                        last.then_inc(s_op, 1)
                    for c in due(at["in_proj"], u) if front else ():
                        if c == 1:
                            pe.wait_ge(s_zc, 2 * A + 1)
                        elif back:
                            pe.wait_ge(s_gts, 2 * F + 2)
                        else:
                            pe.wait_ge(s_tap, 6 * j + 6)
                        in_proj(A, 1 - par, c)
                    if u == at["turn_x1"] and back:
                        if front:
                            pe.wait_ge(s_zc, 2 * A + 2)
                        pe.wait_ge(s_x1, F + 1)
                        for t in range(NT):
                            last = nc.tensor.transpose(tile_of(BX1, t), x1[:, t, :], ident[:])
                        last.then_inc(s_x1t, 1)
                    for part in due(at["gate_up"], u) if back else ():
                        if part == 0:
                            pe.wait_ge(s_r1, F + 1)
                            pe.wait_ge(s_x1l, F + 1)
                            for m in (0, 1):
                                ffn_in(BGATE[m], w1_hl, m).then_inc(s_ga, 1)
                        if part == 1:
                            if front:
                                pe.wait_ge(s_tap, 6 * A + 6)
                            for m in (0, 1):
                                ffn_in(BUP[m], w2_hl, m).then_inc(s_up, 1)
                        if part == 2:
                            for m in (2, 3):
                                pe.wait_ge(s_sg, 4 * F + m - 1)
                                ffn_in(BGATE[m % 2], w1_hl, m).then_inc(s_ga, 1)
                        if part == 3:
                            for m in (2, 3):
                                pe.wait_ge(s_hid, 4 * F + m - 1)
                                ffn_in(BUP[m % 2], w2_hl, m).then_inc(s_up, 1)
                    if u == at["bcdt"] and front:
                        if back:
                            pe.wait_ge(s_sg, 4 * F + 3)
                        else:
                            pe.wait_ge(s_pre, 4 * j + 4)
                        bcdt_proj(A, 1 - par)
                    if u == at["dt_row"] and front:
                        dt_broadcast(A, 1 - par)
                    for m, part in (divmod(i, 2) for i in due(at["h1"], u)) if back else ():
                        if part == 0:
                            if m == 0:
                                pe.wait_ge(s_sg, 4 * F + 4)
                            elif m < 3:
                                pe.wait_ge(s_hid, 4 * F + 2 + m)
                            elif front:
                                pe.wait_ge(s_pre, 4 * A + 4)
                        hidden(h1_hl, m, part, hid, s_hh, s_hl, s_h1, F)
                    for m, part in (divmod(i, 2) for i in due(at["h2"], u)) if back else ():
                        if part == 0:
                            pe.wait_ge(s_g1f, 4 * F + 1 + m)
                        hidden(h2_hl, m, part, g1, s_g1h, s_g1l, s_h2, F)

            rounds(pe, run)


def kernel(L0_attn_x, L0_attn_W_in, L0_attn_conv_w, L0_attn_conv_b, L0_attn_W_x, L0_attn_A_log, L0_attn_D_param,
           L0_attn_W_dt, L0_attn_b_dt, L0_attn_W_out, L0_ffn_w1_w, L0_ffn_w1_s, L0_ffn_w2_w, L0_ffn_w2_s,
           L0_ffn_h1_w, L0_ffn_h1_s, L0_ffn_h2_w, L0_ffn_h2_s, L0_ffn_w3_w, L0_ffn_w3_s):
    import concourse.bacc as _bacc
    from concourse.bass_utils import run_bass_kernel_spmd as _run

    def arr(a):
        return np.asarray(a)

    def chan(a, k):
        return arr(a).reshape(NC, P, k).transpose(1, 0, 2)

    x = arr(L0_attn_x).reshape(SEQS * SEQ, DM)
    chp = np.concatenate([chan(L0_attn_conv_w, TAPS), chan(L0_attn_conv_b, 1), chan(L0_attn_A_log, NS),
                          chan(L0_attn_D_param, 1), chan(L0_attn_W_dt, 1), chan(L0_attn_b_dt, 1)], axis=2)
    scales = np.stack([arr(s).reshape(NH, P).T for s in (L0_ffn_w1_s, L0_ffn_w2_s, L0_ffn_h1_s, L0_ffn_h2_s)], axis=1)
    ins = {
        "xT": x.T, "xtok": x, "win": arr(L0_attn_W_in).T, "wx": arr(L0_attn_W_x).T, "chp": chp,
        "wout": arr(L0_attn_W_out).T, "w1": arr(L0_ffn_w1_w).T, "w2": arr(L0_ffn_w2_w).T,
        "h1": arr(L0_ffn_h1_w).T, "h2": arr(L0_ffn_h2_w).T, "w3": arr(L0_ffn_w3_w).T, "scales": scales,
        "w3s": arr(L0_ffn_w3_s).reshape(1, DM), "ident_in": np.eye(P, dtype=np.float32),
    }
    nc = _bacc.Bacc("TRN2", target_bir_lowering=False, num_devices=1)
    arrays, args = {}, {}
    for name, a in ins.items():
        arrays[f"{name}_d"] = np.ascontiguousarray(a)
        args[name] = nc.dram_tensor(f"{name}_d", list(a.shape), mybir.dt.from_np(arrays[f"{name}_d"].dtype),
                                    kind="ExternalInput").ap()
    args["out"] = nc.dram_tensor("out_d", [SEQS * SEQ, DM], F32, kind="ExternalOutput").ap()
    build(nc, **args)
    r = _run(nc, [arrays], core_ids=[0])
    return r.results[0]["out_d"].reshape(SEQS, SEQ, DM)
```
